# Optimizing a Trainium2 kernel written in Bass

```python
import numpy as np
import jax
import jax.numpy as jnp

def _softmax(x, axis=-1):
    return jax.nn.softmax(x, axis=axis)

def _gelu(x):
    return jax.nn.gelu(x, approximate=True)

def _silu(x):
    return jax.nn.silu(x)

def _sigmoid(x):
    return jax.nn.sigmoid(x)

def _layernorm(x, axis=-1, eps=1e-05):
    m = jnp.mean(x, axis=axis, keepdims=True)
    v = jnp.var(x, axis=axis, keepdims=True)
    return (x - m) / jnp.sqrt(v + eps)

def _scatter_add(tgt, idx, src, axis=0):
    return tgt.at[idx].add(src)

def _segment_sum(src, seg, n):
    return jax.ops.segment_sum(src, seg, n)
kernel_name = 'mk_cond_resid_d2_seqx_r2_710a6b'

def setup_inputs(seed: int=0):
    np.random.seed(seed)
    _w = jnp.asarray

    def _rec_inputs():
        import jax
        import jax.numpy as jnp
        _rk = jax.random.key(seed)
        x = -0.0002919 + 1 * jax.random.normal(jax.random.fold_in(_rk, 1), (8, 512, 512), jnp.float32)
        _lenS = 512 - jax.random.randint(jax.random.fold_in(_rk, 7), (8,), 0, max(1, 512 // 4) + 1, jnp.int32)
        _lenS2 = 512 - jax.random.randint(jax.random.fold_in(_rk, 8), (8,), 0, max(1, 512 // 4) + 1, jnp.int32)
        cond_1024 = 0.0061147 + 1.02565 * jax.random.normal(jax.random.fold_in(_rk, 11), (8, 512), jnp.float32)
        _validS = jnp.arange(512)[None, :] < _lenS[:, None]
        _validS2 = jnp.arange(512)[None, :] < _lenS2[:, None]
        _causal = jnp.tril(jnp.ones((512, 512), dtype=bool))
        mask_Bx1x1xS_ff0 = jnp.where(jnp.ones((8, 1, 1, 512), dtype=bool), 0.0, -1000000000.0).astype(jnp.float32)
        return (x, cond_1024, mask_Bx1x1xS_ff0)
    x, cond_1024, mask_Bx1x1xS_ff0 = _rec_inputs()

    def _L0_cond_setup():
        import jax, jax.numpy as jnp
        import numpy as np
        EMBED = 512
        HEADS = 16
        HDIM = EMBED // HEADS
        MASK_OUT = -10000.0

        def _split_heads(t):
            B, T, _ = t.shape
            return t.reshape(B, T, HEADS, HDIM).transpose(0, 2, 1, 3)
        key = jax.random.key(seed)
        ks = jax.random.split(key, 12)
        B, S = (4, 1023)
        scale = 0.02
        return {'word_hidden_states': jax.random.normal(ks[0], (B, S, EMBED), jnp.float32), 'image_hidden_states': jax.random.normal(ks[1], (B, EMBED), jnp.float32), 'attention_mask': jnp.zeros((B, 1, 1, S), jnp.float32), 'c_attn_w': jax.random.normal(ks[2], (EMBED, 3 * EMBED), jnp.float32) * scale, 'c_attn_b': jnp.zeros((3 * EMBED,), jnp.float32), 'c_proj_w': jax.random.normal(ks[3], (EMBED, EMBED), jnp.float32) * scale, 'c_proj_b': jnp.zeros((EMBED,), jnp.float32), 'uk_w': jax.random.normal(ks[4], (EMBED, EMBED), jnp.float32) * scale, 'uk_b': jnp.zeros((EMBED,), jnp.float32), 'uv_w': jax.random.normal(ks[5], (EMBED, EMBED), jnp.float32) * scale, 'uv_b': jnp.zeros((EMBED,), jnp.float32)}
    _L0_cond_all = _L0_cond_setup()
    _L0_cond_in = {k: v for k, v in _L0_cond_all.items() if k in ('c_attn_w', 'c_attn_b', 'c_proj_w', 'c_proj_b', 'uk_w', 'uk_b', 'uv_w', 'uv_b')}
    del _L0_cond_all

    def _L1_cond_setup():
        import jax, jax.numpy as jnp
        import numpy as np
        N, T, D, H = (64, 256, 512, 512)
        key = jax.random.key(seed)
        k1, k2, k3, k4 = jax.random.split(key, 4)
        x = jax.random.normal(k1, (N, T, D), dtype=jnp.float32)
        h0 = jax.random.normal(k2, (N, H), dtype=jnp.float32)
        Wx = jax.random.normal(k3, (D, H), dtype=jnp.float32) / np.sqrt(D)
        Wh = jax.random.normal(k4, (H, H), dtype=jnp.float32) / np.sqrt(H)
        b = jnp.zeros((H,), dtype=jnp.float32)
        return {'x': x, 'h0': h0, 'Wx': Wx, 'Wh': Wh, 'b': b}
    _L1_cond_all = _L1_cond_setup()
    _L1_cond_in = {k: v for k, v in _L1_cond_all.items() if k in ('Wx', 'Wh', 'b')}
    del _L1_cond_all
    return {'x': x, 'cond_1024': cond_1024, 'mask_Bx1x1xS_ff0': mask_Bx1x1xS_ff0, 'L0_cond_c_attn_w': _L0_cond_in['c_attn_w'], 'L0_cond_c_attn_b': _L0_cond_in['c_attn_b'], 'L0_cond_c_proj_w': _L0_cond_in['c_proj_w'], 'L0_cond_c_proj_b': _L0_cond_in['c_proj_b'], 'L0_cond_uk_w': _L0_cond_in['uk_w'], 'L0_cond_uk_b': _L0_cond_in['uk_b'], 'L0_cond_uv_w': _L0_cond_in['uv_w'], 'L0_cond_uv_b': _L0_cond_in['uv_b'], 'L1_cond_Wx': _L1_cond_in['Wx'], 'L1_cond_Wh': _L1_cond_in['Wh'], 'L1_cond_b': _L1_cond_in['b']}

def reference(x, cond_1024, mask_Bx1x1xS_ff0, L0_cond_c_attn_w, L0_cond_c_attn_b, L0_cond_c_proj_w, L0_cond_c_proj_b, L0_cond_uk_w, L0_cond_uk_b, L0_cond_uv_w, L0_cond_uv_b, L1_cond_Wx, L1_cond_Wh, L1_cond_b):
    import jax
    import jax.numpy as jnp

    def _L0_cond_ref(word_hidden_states, image_hidden_states, attention_mask, c_attn_w, c_attn_b, c_proj_w, c_proj_b, uk_w, uk_b, uv_w, uv_b):
        import jax, jax.numpy as jnp
        import numpy as np
        EMBED = 512
        HEADS = 16
        HDIM = EMBED // HEADS
        MASK_OUT = -10000.0

        def _split_heads(t):
            B, T, _ = t.shape
            return t.reshape(B, T, HEADS, HDIM).transpose(0, 2, 1, 3)
        B, S, _ = word_hidden_states.shape
        qkv = word_hidden_states @ c_attn_w + c_attn_b
        q_word, k_word, v_word = jnp.split(qkv, 3, axis=-1)
        img = image_hidden_states[:, None, :]
        k_img = img @ uk_w.T + uk_b
        v_img = img @ uv_w.T + uv_b
        k = jnp.concatenate([k_img, k_word], axis=1)
        v = jnp.concatenate([v_img, v_word], axis=1)
        q = _split_heads(q_word)
        k = _split_heads(k)
        v = _split_heads(v)
        scores = jnp.einsum('bhqd,bhkd->bhqk', q, k) / jnp.sqrt(jnp.float32(HDIM))
        qi = jnp.arange(S)[:, None]
        kj = jnp.arange(S + 1)[None, :]
        causal = kj <= qi + 1
        scores = jnp.where(causal[None, None], scores, jnp.float32(MASK_OUT))
        zero_col = jnp.zeros(attention_mask.shape[:-1] + (1,), attention_mask.dtype)
        mask = jnp.concatenate([zero_col, attention_mask], axis=-1)
        scores = scores + mask
        attn = jax.nn.softmax(scores, axis=-1)
        out = jnp.einsum('bhqk,bhkd->bhqd', attn, v)
        out = out.transpose(0, 2, 1, 3).reshape(B, S, EMBED)
        out = out @ c_proj_w + c_proj_b
        return out

    def _L1_cond_ref(x, h0, Wx, Wh, b):
        import jax, jax.numpy as jnp
        import numpy as np
        N, T, D, H = (64, 256, 512, 512)
        xw = jnp.einsum('ntd,dh->nth', x, Wx) + b

        def step(prev_h, xw_t):
            next_h = jnp.tanh(prev_h @ Wh + xw_t)
            return (next_h, next_h)
        _, hs = jax.lax.scan(step, h0, jnp.swapaxes(xw, 0, 1))
        return jnp.swapaxes(hs, 0, 1)
    x = x + _L0_cond_ref(x, cond_1024, mask_Bx1x1xS_ff0, L0_cond_c_attn_w, L0_cond_c_attn_b, L0_cond_c_proj_w, L0_cond_c_proj_b, L0_cond_uk_w, L0_cond_uk_b, L0_cond_uv_w, L0_cond_uv_b)
    x = x + _L1_cond_ref(x, cond_1024, L1_cond_Wx, L1_cond_Wh, L1_cond_b)
    return x

_drawn_inputs = setup_inputs


def setup_inputs(seed=0):
    import zlib

    import numpy as np

    out = dict(_drawn_inputs(seed))
    spreads = {'L0_cond_c_attn_b': (0.0, 0.1),
     'L0_cond_c_proj_b': (0.0, 0.1),
     'L0_cond_uk_b': (0.0, 2.0),
     'L0_cond_uv_b': (0.0, 0.8),
     'L1_cond_b': (0.0, 0.1)}
    factors = {'L0_cond_uk_w': 8.0, 'L0_cond_uv_w': 7.353}
    for name, (base, spread) in spreads.items():
        noise = np.random.default_rng([zlib.crc32(name.encode()), seed]).standard_normal(out[name].shape)
        drawn = base * np.exp(spread * noise) if base else spread * noise
        out[name] = jnp.asarray(drawn.astype(out[name].dtype))
    for name, factor in factors.items():
        out[name] = (out[name] * factor).astype(out[name].dtype)
    return out
```

```python
from contextlib import ExitStack

import concourse.bass as bass
from concourse import mybir

P = 128
Q = 32
B = 8
S = 512
D = 512
H = 16
DH = D // H
C = D // P
HC = H // C
BLOCKS = S // P
PAIRS = B // 2
UNITS = 2 * H
STEPS = S // (BLOCKS * PAIRS)
HALF = STEPS // 2
SCALE = DH ** -0.5
ROOT = DH ** 0.5
BANK = 512
KEYLAG, PVLAG = 2, 3

F32 = mybir.dt.float32
ALU = mybir.AluOpType
ACT = mybir.ActivationFunctionType

LEAD = 4
KV_STORES = 64 * PAIRS * (BLOCKS - 1)
WEIGHT_LOADS = 16 * 9


def order(p):
    if p == BLOCKS:
        pieces = []
    else:
        n = p + 1
        pieces = [("xt", e, 0.5) for e in range(2)]
        pieces += [("q", c, 1.8) for c in range(C)] + [("k", c, 1.8) for c in range(C)]
        pieces += [("v", e, 3.5) for e in range(2)] + [("imgscore", e, 1.7) for e in range(2)]
        for u in range(UNITS + PVLAG):
            w = 0.22 * n * (u < UNITS) + 0.12 * n * (KEYLAG <= u < UNITS + KEYLAG) + 0.1 * n * (u >= PVLAG)
            pieces.append(("head", u, w))
            if u % H == 0 and u:
                pieces.append(("imgprob", u // H - 1, 1.0))
            if u % H == PVLAG - 1 and u >= H:
                pieces.append(("norm", u // H - 1, 1.7))
        pieces += [("proj", c, 1.8) for c in range(C)] + [("wx", c, 1.8) for c in range(C)]
        pieces += [("x1n", e, 0.5) for e in range(2)]
    events = []
    total = sum(w for _, _, w in pieces) or 1
    done, step = 0.0, 0

    def steps_until(last):
        nonlocal step
        while step < last:
            events.append(("step", step))
            step += 1
            if step == HALF + 2:
                events.append(("out", 0))

    for kind, i, w in pieces:
        events.append((kind, i))
        done += w
        if p:
            steps_until(min(STEPS, int(STEPS * done / total + 1e-6)))
    if p:
        steps_until(STEPS)
        events.append(("out", 1))
    return events


JOBS = ("xt", "q", "k", "v", "imgscore", "proj", "wx", "x1n", "out")


def jobs(p):
    n, out = 0, {}
    for kind, i in order(p):
        for name in ([kind] if kind in JOBS else ["pimgt", "rbc"] if kind == "imgprob" else []):
            out[name, i] = n
            n += 1
    assert n % 2 == 0
    out["count"] = n
    return out


def attention_recurrence(nc, x, cond, mask, w_qkv, b_qk, b_v, w_proj, b_proj, uk_w, uk_b, uv_w, uv_b,
                         w_x, w_h, b_h, ident_in, causal_in, headmask_in, out):
    JOB = [jobs(p) for p in range(BLOCKS + 1)]
    base = [0]
    for p in range(BLOCKS):
        base.append(base[-1] + PAIRS * JOB[p]["count"])

    with ExitStack() as ctx:
        def sb(name, shape, dt=F32):
            return ctx.enter_context(nc.sbuf_tensor(name, shape, dt))

        def sem(name):
            return ctx.enter_context(nc.semaphore(name))

        wqkv = sb("wqkv", [P, C, 3 * D])
        wproj = sb("wproj", [P, C, D])
        wx = sb("wx", [P, C, D])
        wh = sb("wh", [P, C, D])
        bqk = sb("bqk", [P, 2, C])
        bv = sb("bv", [P, D])
        bproj = sb("bproj", [P, C])
        bx = sb("bx", [P, C])
        ukb = sb("ukb", [P, C])
        ident = sb("ident", [P, P])
        causal = sb("causal", [P, P])
        xin = sb("xin", [P, 2, D])
        xT = sb("xT", [P, C, 2 * P])
        qT = sb("qT", [P, C, 2 * P])
        qpad = sb("qpad", [P, 2, C, HC, P])
        kst = sb("kst", [P, 2, C, S])
        vst = sb("vst", [P, 2, BLOCKS, D])
        msk = sb("msk", [P, 2, S])
        kimg = sb("kimg", [P, C, B, HC])
        vimg = sb("vimg", [H, 2, D])
        probs = sb("probs", [P, 3, S])
        probsT = sb("probsT", [P, 2, S])
        nmax = sb("nmax", [P, 2, H])
        nimg = sb("nimg", [P, 2, H])
        rowsum = sb("rowsum", [P, 2, H])
        dimg = sb("dimg", [P, 2, H])
        pimg = sb("pimg", [P, 2, H])
        total = sb("total", [P, 2, H])
        rinv = sb("rinv", [P, 2, H])
        pimgT = sb("pimgT", [H, P])
        rbc = sb("rbc", [P, C, P])
        rinvx = sb("rinvx", [P, H, Q])
        attnT = sb("attnT", [P, C, 2 * P])
        x1T = sb("x1T", [P, C, 2 * P])
        x1nat = sb("x1nat", [P, 2, D])
        xw = sb("xw", [P, 2, C, B, P])
        pre = sb("pre", [P, C, Q])
        hist = sb("hist", [P, 2, C, B, HALF])
        x1out = sb("x1out", [P, D])
        osb = sb("osb", [P, D])
        cond_sb = sb("cond_sb", [B, D])
        imgT = sb("imgT", [P, C, B])
        imgTx = rbc[:].rearrange("p f (b h) -> p f b h", b=B)

        dense = [ctx.enter_context(nc.psum_tensor(f"dense{i}", [P, BANK], F32)) for i in range(2)]
        scores = [ctx.enter_context(nc.psum_tensor(f"scores{i}", [P, BANK], F32)) for i in range(2)]
        turned = [ctx.enter_context(nc.psum_tensor(f"turned{i}", [P, BANK], F32)) for i in range(2)]
        pv = ctx.enter_context(nc.psum_tensor("pv", [P, BANK], F32))
        rec = ctx.enter_context(nc.psum_tensor("rec", [P, BANK], F32))

        headmask = xT[:, 0:2, :].rearrange("p a n -> p (a n)")
        pre_all = pre[:].rearrange("p f q -> p (f q)")

        k_dram = nc.dram_tensor("k_dram", [B, P, C, S], F32, kind="Internal").ap()
        v_dram = nc.dram_tensor("v_dram", [B, S, D], F32, kind="Internal").ap()
        vimg_dram = nc.dram_tensor("vimg_dram", [B, H, D], F32, kind="Internal").ap()
        x1_dram = nc.dram_tensor("x1_dram", [B, S, D], F32, kind="Internal").ap()

        weights_loaded = sem("weights_loaded")
        setup_loaded = sem("setup_loaded")
        setup_turned = sem("setup_turned")
        setup_copied = sem("setup_copied")
        setup_product = sem("setup_product")
        zeroed = sem("zeroed")
        image_ready = sem("image_ready")
        kimg_ready = sem("kimg_ready")
        x_loaded = sem("x_loaded")
        staged = [sem(f"staged{e}") for e in range(2)]
        mask_scaled = sem("mask_scaled")
        mask_ready = sem("mask_ready")
        qpad_ready = sem("qpad_ready")
        dense_ready = sem("dense_ready")
        dense_copied = [sem(f"dense_copied{i}") for i in range(2)]
        scores_ready = sem("scores_ready")
        shifted_ready = sem("shifted_ready")
        probs_ready = sem("probs_ready")
        turned_ready = sem("turned_ready")
        turned_copied = [sem(f"turned_copied{i}") for i in range(2)]
        pv_done = sem("pv_done")
        dimg_ready = sem("dimg_ready")
        pimg_ready = sem("pimg_ready")
        total_ready = sem("total_ready")
        recip_ready = sem("recip_ready")
        rinv_ready = sem("rinv_ready")
        attn_summed = sem("attn_summed")
        attn_ready = sem("attn_ready")
        kv_stored = sem("kv_stored")
        x1_stored = sem("x1_stored")
        x1out_loaded = sem("x1out_loaded")
        rec_ready = sem("rec_ready")
        rec_turned = sem("rec_turned")
        pre_ready = sem("pre_ready")
        h_ready = sem("h_ready")
        out_stored = sem("out_stored")

        def folded(ap):
            return ap.rearrange("p (j f c) -> p f j c", j=C, f=C)

        def trip(p, r):
            return r + PAIRS * p

        def job(p, r, name, i):
            return r * JOB[p]["count"] + (base[p] + JOB[p][name, i])

        def wait_dense(eng, p, r, name, i):
            eng.wait_ge(dense_ready, job(p, r, name, i) + 1)

        def wait_copied(eng, p, r, name, i):
            n = JOB[p][name, i]
            eng.wait_ge(dense_copied[n % 2], since(r * (JOB[p]["count"] // 2) + (base[p] // 2 + n // 2 + 1)))

        def wait_bank(eng, p, r, name, i):
            n = JOB[p][name, i]
            eng.wait_ge(dense_copied[n % 2], since(r * (JOB[p]["count"] // 2) + (base[p] // 2 + n // 2)))

        def bank(p, name, i):
            return dense[JOB[p][name, i] % 2]

        def copied(p, name, i):
            return dense_copied[JOB[p][name, i] % 2]

        def staged_by(p, r):
            return r * 32 + 32 if p == 0 else r * 64 + (PAIRS * 32 + (p - 1) * PAIRS * 64 + 64)

        def step_count(p, r, s):
            return r * STEPS + ((p - 1) * PAIRS * STEPS + s)

        def since(n):
            return n + LEAD

        def after_vimg(n):
            return n + 16

        def alone(eng):
            eng.nop(nofuse=True)

        block = ctx.enter_context(nc.Block())

        @block.sync
        def _(sp):
            sp.dma_start(ident[:], ident_in).then_inc(setup_loaded, 16)
            sp.dma_start(cond_sb[:], cond).then_inc(setup_loaded, 16)
            sp.dma_start(kst[:, 0, :, :], uk_w).then_inc(setup_loaded, 16)
            sp.dma_start(kst[:, 1, :, :], uv_w).then_inc(setup_loaded, 16)
            sp.dma_start(ukb[:], uk_b).then_inc(setup_loaded, 16)
            sp.dma_start(bv[:], uv_b.rearrange("(a n) -> a n", a=1).broadcast_to([P, D])).then_inc(setup_loaded, 16)
            sp.dma_start(headmask, headmask_in).then_inc(setup_loaded, 16)
            for tile, w in ((wqkv, w_qkv), (wproj, w_proj), (wx, w_x), (wh, w_h)):
                sp.dma_start(tile[:], w).then_inc(weights_loaded, 16)
            for tile, b in ((bqk, b_qk), (bproj, b_proj), (bx, b_h)):
                sp.dma_start(tile[:], b).then_inc(weights_loaded, 16)
            sp.dma_start(causal[:], causal_in).then_inc(weights_loaded, 16)
            sp.wait_ge(image_ready, 1)
            sp.dma_start(bv[:], b_v.rearrange("(a n) -> a n", a=1).broadcast_to([P, D])
                         ).then_inc(weights_loaded, 16)
            for stored in (kv_stored, x1_stored, out_stored):
                sp.wait_ge(stored, after_vimg(0))

            for p in range(BLOCKS):
                with sp.Fori(0, PAIRS) as r:
                    g = trip(p, r)
                    sp.wait_ge(attn_summed, since(g * 2))
                    for e in range(2):
                        sp.dma_start(xin[:, e, :], x[bass.ds(r * 2 + e, 1), P * p:P * p + P, :]).then_inc(x_loaded, 16)
                    sp.wait_ge(kv_stored, after_vimg(g * 64) if p < BLOCKS - 1 else after_vimg(KV_STORES))
                    for e in range(2):
                        batch = bass.ds(r * 2 + e, 1)
                        sp.dma_start(msk[:, e, 0:P * (p + 1)], mask[batch, 0, 0, 0:P * (p + 1)]
                                     .broadcast_to([P, P * (p + 1)])).then_inc(staged[e], 16)
                        sp.dma_start(vimg[:, e, :], vimg_dram[batch, :, :]).then_inc(staged[e], 16)
                        if p:
                            sp.dma_start(kst[:, e, :, 0:P * p], k_dram[batch, :, :, 0:P * p]).then_inc(staged[e], 16)
                            sp.dma_start(vst[:, e, 0:p, :], v_dram[batch, 0:P * p, :]
                                         .rearrange("a (n q) d -> a q n d", q=P)).then_inc(staged[e], 16)

        @block.gpsimd
        def _(pool):
            for lead in [*dense_copied, *turned_copied, shifted_ready, turned_ready, pv_done, attn_summed,
                         attn_ready]:
                pool.sem_inc(lead, LEAD)
            pool.memset(qpad[:], 0.0).then_inc(zeroed, 1)
            pool.wait_ge(image_ready, 2)
            for rows, stored in ((slice(0, 3 * Q // 2), kv_stored), (slice(3 * Q // 2, 3 * Q), x1_stored),
                                 (slice(3 * Q, P), out_stored)):
                pool.dma_start(vimg_dram.rearrange("b h d -> (b h) d")[rows, :], xin[rows, 0, :]).then_inc(stored, 16)
            pool.wait_ge(zeroed, 1)
            pool.wait_ge(weights_loaded, WEIGHT_LOADS)

            def load_x1(p, r, k):
                pool.dma_start(x1out[:], x1_dram[:, bass.ds(r * STEPS + ((p - 1) * P + k * HALF), HALF), :]
                               ).then_inc(x1out_loaded, 16)

            for p in range(BLOCKS + 1):
                if p:
                    pool.wait_ge(x1_stored, after_vimg(p * PAIRS * 32))
                with pool.Fori(0, PAIRS) as r:
                    g = trip(p, r)
                    for kind, i in order(p):
                        if kind == "xt" and i == 0:
                            for e in range(2):
                                pool.wait_ge(staged[e], staged_by(p, r))
                                alone(pool)
                                pool.tensor_scalar(msk[:, e, 0:P * (p + 1)], msk[:, e, 0:P * (p + 1)], ROOT, None,
                                                   ALU.mult).then_inc(mask_scaled, 1)
                                pool.wait_ge(mask_scaled, g * 2 + (e + 1))
                                pool.tensor_tensor(msk[:, e, P * p:P * (p + 1)], msk[:, e, P * p:P * (p + 1)],
                                                   causal[:], ALU.add).then_inc(mask_ready, 1)
                        elif kind == "head" and i == 2 and p < BLOCKS - 1:
                            for e in range(2):
                                wait_copied(pool, p, r, "v", e)
                            alone(pool)
                            for e in range(2):
                                batch = bass.ds(r * 2 + e, 1)
                                pool.dma_start(k_dram[batch, :, :, P * p:P * p + P],
                                               kst[:, e, :, P * p:P * p + P]).then_inc(kv_stored, 16)
                                pool.dma_start(v_dram[batch, P * p:P * p + P, :], vst[:, e, p, :]).then_inc(kv_stored, 16)
                        elif kind == "x1n":
                            wait_copied(pool, p, r, "x1n", i)
                            alone(pool)
                            pool.dma_start(x1_dram[bass.ds(r * 2 + i, 1), P * p:P * p + P, :],
                                           x1nat[:, i, :]).then_inc(x1_stored, 16)
                        elif kind == "step" and i == 0:
                            load_x1(p, r, 0)
                        elif kind == "out":
                            wait_copied(pool, p, r, "out", i)
                            alone(pool)
                            pool.dma_start(out[:, bass.ds(r * STEPS + ((p - 1) * P + i * HALF), HALF), :], osb[:]
                                           ).then_inc(out_stored, 16)
                            if i == 0:
                                load_x1(p, r, 1)
            pool.wait_ge(out_stored, after_vimg(16 * 2 * PAIRS * BLOCKS))
            pool.wait_ge(kv_stored, after_vimg(KV_STORES))
            pool.wait_ge(x1_stored, after_vimg(32 * PAIRS * BLOCKS))

        @block.scalar
        def _(act):
            act.wait_ge(weights_loaded, WEIGHT_LOADS)
            for p in range(BLOCKS + 1):
                n = P * (p + 1)

                def head(r, u):
                    g = trip(p, r)
                    if KEYLAG <= u < UNITS + KEYLAG and u % 2:
                        v = u - KEYLAG
                        act.wait_ge(turned_ready, since(g * UNITS + (v + 1)))
                        act.wait_ge(pv_done, since(g * UNITS + (v - 1)))
                        act.copy(probsT[:, 1, 0:n], turned[1][:, 0:n]).then_inc(turned_copied[1], 1)
                    if u < UNITS:
                        e, h = divmod(u, H)
                        act.wait_ge(shifted_ready, since(g * UNITS + (u + 1)))
                        act.activation(probs[:, u % 3, 0:n], probs[:, u % 3, 0:n], ACT.Exp, scale=-1.0,
                                       bias=nmax[:, e, h:h + 1], accum_out=rowsum[:, e, h:h + 1]).then_inc(probs_ready, 1)

                with act.Fori(0, PAIRS) as r:
                    g = trip(p, r)
                    for kind, i in order(p):
                        if kind == "xt":
                            wait_dense(act, p, r, "xt", i)
                            act.copy(xT[:, :, P * i:P * i + P],
                                     bank(p, kind, i)[:, :].rearrange("p (f t) -> p f t", f=C)
                                     ).then_inc(copied(p, kind, i), 1)
                        elif kind == "q":
                            wait_dense(act, p, r, "q", i)
                            act.activation(qT[:, i, :], bank(p, kind, i)[:, 0:2 * P], ACT.Identity,
                                           bias=bqk[:, 0, i:i + 1]).then_inc(copied(p, kind, i), 1)
                        elif kind == "head":
                            head(r, i)
                        elif kind == "imgprob":
                            act.wait_ge(dimg_ready, g * 2 + (i + 1))
                            act.activation(pimg[:, i, :], dimg[:, i, :], ACT.Exp).then_inc(pimg_ready, 1)
                            wait_dense(act, p, r, "pimgt", i)
                            act.copy(pimgT[:], bank(p, "pimgt", i)[0:H, 0:P]).then_inc(copied(p, "pimgt", i), 1)
                            wait_dense(act, p, r, "rbc", i)
                            act.copy(rbc[:].rearrange("p c q -> p (c q)"), bank(p, "rbc", i)[:, :]
                                     ).then_inc(copied(p, "rbc", i), 1)
                        elif kind == "wx":
                            wait_dense(act, p, r, "wx", i)
                            act.activation(xw[:, p % 2, i, bass.ds(r * 2, 2), :],
                                           bank(p, kind, i)[:, 0:2 * P].rearrange("p (e t) -> p e t", e=2),
                                           ACT.Identity, bias=bx[:, i:i + 1]).then_inc(copied(p, kind, i), 1)
                        elif kind == "x1n":
                            wait_dense(act, p, r, "x1n", i)
                            act.wait_ge(x1_stored, after_vimg(g * 32))
                            act.copy(folded(x1nat[:, i, :]),
                                     bank(p, kind, i)[:, :].rearrange("p (f j c) -> p f j c", f=C, j=C)
                                     ).then_inc(copied(p, kind, i), 1)
                        elif kind == "step":
                            act.wait_ge(pre_ready, step_count(p, r, i) + 1)
                            act.activation(hist[:, i // HALF, :, :, i % HALF], pre[:, :, 0:B], ACT.Tanh).then_inc(h_ready, 1)

        @block.vector
        def _(dve):
            dve.memset(rec[:], 0.0).then_inc(zeroed, 1)
            dve.memset(kimg[:], 0.0).then_inc(zeroed, 1)
            dve.wait_ge(zeroed, 3)
            for e, banks in ((0, scores + turned), (1, dense + [pv, scores[1]])):
                for f in range(C):
                    dve.wait_ge(setup_turned, e * C + f + 1)
                    dve.tensor_copy(vst[:, e, f, :], banks[f][:, :]).then_inc(setup_copied, 1)
            dve.wait_ge(setup_turned, 2 * C + 1)
            dve.tensor_copy(imgT[:], scores[0][:, 0:C * B].rearrange("p (f b) -> p f b", f=C)).then_inc(setup_copied, 1)
            dve.tensor_copy(hist[:, 1, :, :, HALF - 1],
                            scores[0][:, 0:C * B].rearrange("p (f b) -> p f b", f=C)).then_inc(h_ready, 1)
            dve.wait_ge(setup_copied, 2 * C + 1)
            dve.tensor_copy(imgTx, imgT[:].unsqueeze(3).broadcast_to([P, C, B, H])).then_inc(setup_copied, 1)
            dve.wait_ge(setup_product, 1)
            for j in range(HC):
                rows = slice(Q * j, Q * j + Q)
                dve.tensor_tensor(kimg[rows, :, :, j], scores[1][rows, 0:C * B].rearrange("p (c b) -> p c b", c=C),
                                  ukb[rows, :].unsqueeze(2).broadcast_to([Q, C, B]), ALU.add).then_inc(kimg_ready, 1)
            dve.wait_ge(setup_product, 2)
            dve.tensor_tensor(xin[:, 1, :], turned[0][:, :], bv[:], ALU.add).then_inc(image_ready, 1)
            dve.wait_ge(image_ready, 1)
            dve.tensor_tensor(xin[:, 0, :], xin[:, 1, :], headmask, ALU.mult).then_inc(image_ready, 1)
            dve.wait_ge(weights_loaded, WEIGHT_LOADS)

            for p in range(BLOCKS + 1):
                n = P * (p + 1)
                if p:
                    for i in range(2):
                        dve.wait_ge(dense_copied[i], since(base[p] // 2))

                def head(r, u):
                    g = trip(p, r)
                    if u < UNITS:
                        e, h = divmod(u, H)
                        dve.wait_ge(scores_ready, g * UNITS + (u + 1))
                        dve.wait_ge(turned_ready, since(g * UNITS + (u - 2)))
                        if h == 0:
                            dve.wait_ge(mask_ready, g * 2 + (e + 1))
                        alone(dve)
                        dve.tensor_tensor_reduce(out=probs[:, u % 3, 0:n], in0=scores[u % 2][:, 0:n],
                                                 in1=msk[:, e, 0:n], scale=-SCALE, scalar=nimg[:, e, h:h + 1],
                                                 op0=ALU.add, op1=ALU.min, accum_out=nmax[:, e, h:h + 1]
                                                 ).then_inc(shifted_ready, 1)
                    if KEYLAG <= u < UNITS + KEYLAG and u % 2 == 0:
                        v = u - KEYLAG
                        dve.wait_ge(turned_ready, since(g * UNITS + (v + 1)))
                        dve.wait_ge(pv_done, since(g * UNITS + (v - 1)))
                        dve.tensor_copy(probsT[:, 0, 0:n], turned[0][:, 0:n]).then_inc(turned_copied[0], 1)

                with dve.Fori(0, PAIRS) as r:
                    g = trip(p, r)
                    for kind, i in order(p):
                        if kind == "k" and i == 0:
                            wait_copied(dve, p, r, "q", C - 2)
                            wait_copied(dve, p, r, "q", C - 1)
                            for e in range(2):
                                for j in range(HC):
                                    rows = slice(Q * j, Q * j + Q)
                                    dve.tensor_copy(qpad[rows, e, :, j, :],
                                                    qT[rows, :, P * e:P * e + P]).then_inc(qpad_ready, 1)
                        if kind == "k":
                            wait_dense(dve, p, r, "k", i)
                            if i == 0:
                                dve.wait_ge(kv_stored, after_vimg(g * 64) if p < BLOCKS - 1 else after_vimg(KV_STORES))
                            dve.tensor_scalar(kst[:, :, i, P * p:P * p + P],
                                              bank(p, kind, i)[:, 0:2 * P].rearrange("p (e t) -> p e t", e=2),
                                              bqk[:, 1, i:i + 1], None, ALU.add).then_inc(copied(p, kind, i), 1)
                        elif kind == "v":
                            wait_dense(dve, p, r, "v", i)
                            dve.tensor_tensor(vst[:, i, p, :], bank(p, kind, i)[:, :], bv[:], ALU.add
                                              ).then_inc(copied(p, kind, i), 1)
                        elif kind == "imgscore":
                            wait_dense(dve, p, r, "imgscore", i)
                            dve.tensor_scalar(nimg[:, i, :], bank(p, kind, i)[:, 0:H], -SCALE, None, ALU.mult
                                              ).then_inc(copied(p, kind, i), 1)
                            wait_copied(dve, p, r, "imgscore", i)
                        elif kind == "head":
                            head(r, i)
                        elif kind == "imgprob":
                            dve.wait_ge(shifted_ready, since(g * UNITS + (i + 1) * H))
                            dve.tensor_tensor(dimg[:, i, :], nmax[:, i, :], nimg[:, i, :], ALU.subtract
                                              ).then_inc(dimg_ready, 1)
                            dve.wait_ge(pimg_ready, g * 2 + (i + 1))
                            dve.wait_ge(probs_ready, g * UNITS + (i + 1) * H)
                            dve.tensor_tensor(total[:, i, :], rowsum[:, i, :], pimg[:, i, :], ALU.add
                                              ).then_inc(total_ready, 1)
                            dve.wait_ge(total_ready, g * 2 + (i + 1))
                            dve.reciprocal(rinv[:, i, :], total[:, i, :]).then_inc(recip_ready, 1)
                            dve.wait_ge(recip_ready, g * 2 + (i + 1))
                            dve.tensor_copy(rinvx[:], rinv[:, i, :].unsqueeze(2).broadcast_to([P, H, Q])
                                            ).then_inc(rinv_ready, 1)
                        elif kind == "norm":
                            dve.wait_ge(attn_summed, since(g * 2 + (i + 1)))
                            wait_copied(dve, p, r, "rbc", i)
                            dve.tensor_tensor(attnT[:, :, P * i:P * i + P], pv[:, :].rearrange("p (c q) -> p c q", c=C),
                                              rbc[:], ALU.mult).then_inc(attn_ready, 1)
                        elif kind == "proj":
                            wait_dense(dve, p, r, "proj", i)
                            dve.scalar_tensor_tensor(out=x1T[:, i, :], in0=bank(p, kind, i)[:, 0:2 * P],
                                                     scalar=bproj[:, i:i + 1], in1=xT[:, i, :], op0=ALU.add,
                                                     op1=ALU.add).then_inc(copied(p, kind, i), 1)
                        elif kind == "step":
                            t = step_count(p, r, i)
                            dve.wait_ge(rec_ready, t + 1)
                            dve.transpose(pre_all, rec[:, 0:P]).then_inc(rec_turned, 1)
                            dve.wait_ge(rec_turned, t + 1)
                            dve.tensor_tensor(pre[:, :, 0:B], pre[:, :, 0:B],
                                              xw[:, (p - 1) % 2, :, :, bass.ds(r * STEPS + i, 1)].rearrange("p f b a -> p f (b a)"),
                                              ALU.add).then_inc(pre_ready, 1)
                        elif kind == "out":
                            o = r * 2 + ((p - 1) * PAIRS * 2 + i)
                            wait_dense(dve, p, r, "out", i)
                            dve.wait_ge(x1out_loaded, o * 16 + 16)
                            dve.wait_ge(out_stored, after_vimg(o * 16))
                            dve.tensor_tensor(folded(osb[:]),
                                              bank(p, kind, i)[:, :].rearrange("p (f j c) -> p f j c", f=C, j=C),
                                              folded(x1out[:]), ALU.add).then_inc(copied(p, kind, i), 1)

        @block.tensor
        def _(pe):
            pe.wait_ge(setup_loaded, 7 * 16)
            for e, banks in ((0, scores + turned), (1, dense + [pv, scores[1]])):
                for f in range(C):
                    if (e, f) == (1, C - 1):
                        pe.wait_ge(setup_copied, 2)
                    for o in range(C):
                        last = pe.transpose(banks[f][:, P * o:P * o + P], kst[:, e, o, P * f:P * f + P], ident[:])
                    last.then_inc(setup_turned, 1)
            pe.wait_ge(setup_copied, 2 * C)
            for f in range(C):
                last = pe.transpose(scores[0][:, B * f:B * f + B], cond_sb[:, P * f:P * f + P], ident[0:B, 0:B])
            last.then_inc(setup_turned, 1)
            pe.wait_ge(setup_copied, 2 * C + 1)
            for c in range(C):
                for f in range(C):
                    last = pe.matmul(scores[1][:, B * c:B * c + B], vst[:, 0, f, P * c:P * c + P], imgT[:, f, :],
                                     start=f == 0, stop=f == C - 1)
            last.then_inc(setup_product, 1)
            pe.wait_ge(setup_copied, 2 * C + 2)
            for f in range(C):
                last = pe.matmul(turned[0][:, :], rbc[:, f, :], vst[:, 1, f, :],
                                 start=f == 0, stop=f == C - 1)
            last.then_inc(setup_product, 1)
            pe.wait_ge(image_ready, 2)
            pe.wait_ge(kimg_ready, HC)
            pe.wait_ge(h_ready, 1)
            pe.wait_ge(weights_loaded, WEIGHT_LOADS)
            pe.wait_ge(zeroed, 3)

            for p in range(BLOCKS + 1):
                n = P * (p + 1)

                def head(r, u):
                    g = trip(p, r)
                    if u < UNITS:
                        e, h = divmod(u, H)
                        c, j = divmod(h, HC)
                        if h == 0:
                            pe.wait_ge(qpad_ready, g * 2 * HC + (e + 1) * HC)
                            pe.wait_ge(staged[e], staged_by(p, r))
                        pe.wait_ge(shifted_ready, since(g * UNITS + (u - 1)))
                        pe.matmul(scores[u % 2][:, 0:n], qpad[:, e, c, j, :], kst[:, e, c, 0:n], start=True, stop=True
                                  ).then_inc(scores_ready, 1)
                    if KEYLAG <= u < UNITS + KEYLAG:
                        v = u - KEYLAG
                        pe.wait_ge(probs_ready, g * UNITS + (v + 1))
                        pe.wait_ge(turned_copied[v % 2], since(g * H + (v // 2)))
                        for k in range(p + 1):
                            last = pe.transpose(turned[v % 2][:, P * k:P * k + P], probs[:, v % 3, P * k:P * k + P], ident[:])
                        last.then_inc(turned_ready, 1)
                    if u >= PVLAG:
                        v = u - PVLAG
                        e, h = divmod(v, H)
                        c, j = divmod(h, HC)
                        pe.wait_ge(turned_copied[v % 2], since(g * H + (v // 2 + 1)))
                        if h == 0:
                            pe.wait_ge(attn_ready, since(g * 2 + e))
                        for k in range(p + 1):
                            last = pe.matmul(pv[Q * j:Q * j + Q, P * c:P * c + P], vst[:, e, k, DH * h:DH * h + DH],
                                             probsT[:, v % 2, P * k:P * k + P], start=c == 0 and k == 0, stop=False,
                                             skip_group_check=True)
                        last.then_inc(pv_done, 1)

                with pe.Fori(0, PAIRS) as r:
                    g = trip(p, r)
                    for kind, i in order(p):
                        if kind in JOBS and kind != "out":
                            wait_bank(pe, p, r, kind, i)
                            d = bank(p, kind, i)
                        if kind == "xt":
                            pe.wait_ge(x_loaded, g * 32 + 32)
                            for f in range(C):
                                last = pe.transpose(d[:, P * f:P * f + P], xin[:, i, P * f:P * f + P], ident[:])
                            last.then_inc(dense_ready, 1)
                        elif kind in ("q", "k"):
                            if kind == "q" and i == 0:
                                wait_copied(pe, p, r, "xt", 0)
                                wait_copied(pe, p, r, "xt", 1)
                            w0 = D * (kind == "k") + P * i
                            for f in range(C):
                                last = pe.matmul(d[:, 0:2 * P], wqkv[:, f, w0:w0 + P], xT[:, f, :], start=f == 0, stop=f == C - 1)
                            last.then_inc(dense_ready, 1)
                        elif kind == "v":
                            for f in range(C):
                                last = pe.matmul(d[:, :], xT[:, f, P * i:P * i + P], wqkv[:, f, 2 * D:3 * D],
                                                 start=f == 0, stop=f == C - 1)
                            last.then_inc(dense_ready, 1)
                        elif kind == "imgscore":
                            for c in range(C):
                                last = pe.matmul(d[:, HC * c:HC * c + HC], qT[:, c, P * i:P * i + P],
                                                 kimg[:, c, bass.ds(r * 2 + i, 1), :], start=True, stop=True)
                            last.then_inc(dense_ready, 1)
                        elif kind == "head":
                            head(r, i)
                        elif kind == "imgprob":
                            pe.wait_ge(pimg_ready, g * 2 + (i + 1))
                            wait_bank(pe, p, r, "pimgt", i)
                            pe.transpose(bank(p, "pimgt", i)[0:H, 0:P], pimg[:, i, :], ident[:]).then_inc(dense_ready, 1)
                            pe.wait_ge(rinv_ready, g * 2 + (i + 1))
                            wait_bank(pe, p, r, "rbc", i)
                            for c in range(C):
                                last = pe.transpose(bank(p, "rbc", i)[:, P * c:P * c + P],
                                                    rinvx[:, HC * c:HC * c + HC, :].rearrange("p j q -> p (j q)"),
                                                    ident[:])
                            last.then_inc(dense_ready, 1)
                        elif kind == "norm":
                            wait_copied(pe, p, r, "pimgt", i)
                            for c in range(C):
                                last = pe.matmul(pv[:, P * c:P * c + P], vimg[:, i, P * c:P * c + P], pimgT[:],
                                                 start=False, stop=True, skip_group_check=True)
                            last.then_inc(attn_summed, 1)
                        elif kind == "proj":
                            if i == 0:
                                pe.wait_ge(attn_ready, since(g * 2 + 2))
                            for c in range(C):
                                last = pe.matmul(d[:, 0:2 * P], wproj[:, c, P * i:P * i + P], attnT[:, c, :],
                                                 start=c == 0, stop=c == C - 1)
                            last.then_inc(dense_ready, 1)
                        elif kind == "wx":
                            if i == 0:
                                wait_copied(pe, p, r, "proj", C - 2)
                                wait_copied(pe, p, r, "proj", C - 1)
                            for f in range(C):
                                last = pe.matmul(d[:, 0:2 * P], wx[:, f, P * i:P * i + P], x1T[:, f, :],
                                                 start=f == 0, stop=f == C - 1)
                            last.then_inc(dense_ready, 1)
                        elif kind == "x1n":
                            for f in range(C):
                                last = pe.transpose(d[:, P * f:P * f + P], x1T[:, f, P * i:P * i + P], ident[:])
                            last.then_inc(dense_ready, 1)
                        elif kind == "step":
                            pe.wait_ge(h_ready, step_count(p, r, i) + 1)
                            before = (i - 1) % STEPS
                            for f in range(C):
                                for j in range(C):
                                    last = pe.matmul(rec[Q * j:Q * j + B, 0:P], hist[:, before // HALF, f, :, before % HALF],
                                                     wh[:, f, P * j:P * j + P], start=f == 0, stop=f == C - 1)
                            last.then_inc(rec_ready, 1)
                        elif kind == "out":
                            wait_bank(pe, p, r, "out", i)
                            pe.wait_ge(h_ready, r * STEPS + ((p - 1) * PAIRS * STEPS + (i + 1) * HALF + 1))
                            for f in range(C):
                                last = pe.transpose(bank(p, kind, i)[:, P * f:P * f + P],
                                                    hist[:, i, f, :, :].rearrange("p b s -> p (b s)"), ident[:])
                            last.then_inc(dense_ready, 1)


def kernel(x, cond_1024, mask_Bx1x1xS_ff0, L0_cond_c_attn_w, L0_cond_c_attn_b, L0_cond_c_proj_w,
           L0_cond_c_proj_b, L0_cond_uk_w, L0_cond_uk_b, L0_cond_uv_w, L0_cond_uv_b, L1_cond_Wx,
           L1_cond_Wh, L1_cond_b):
    import numpy as np
    import concourse.bacc as bacc
    from concourse.bass_utils import run_bass_kernel_spmd

    inputs = {
        "x": x, "cond": cond_1024, "mask": mask_Bx1x1xS_ff0, "w_qkv": L0_cond_c_attn_w,
        "w_proj": L0_cond_c_proj_w, "b_proj": L0_cond_c_proj_b,
        "uk_w": L0_cond_uk_w, "uk_b": L0_cond_uk_b, "uv_w": L0_cond_uv_w, "uv_b": L0_cond_uv_b,
        "w_x": L1_cond_Wx, "w_h": L1_cond_Wh, "b_h": L1_cond_b,
    }
    b_qkv = L0_cond_c_attn_b

    def folded(a, axis):
        axis %= a.ndim
        cut = a.reshape(a.shape[:axis] + (C, C, Q) + a.shape[axis + 1:])
        return np.swapaxes(cut, axis, axis + 1).reshape(a.shape)

    def chunked(a):
        return np.swapaxes(a.reshape((C, P) + a.shape[1:]), 0, 1)

    inputs["x"] = folded(x, -1)
    inputs["cond"] = folded(cond_1024, -1)
    for name in ("w_qkv", "w_x", "w_h", "b_proj", "b_h"):
        inputs[name] = folded(inputs[name], 0)
    for name in ("w_proj", "w_x", "uk_w", "uv_w"):
        inputs[name] = folded(inputs[name], 1)
    for name in ("w_qkv", "w_proj", "w_x", "w_h", "uk_w", "uv_w", "uk_b", "b_proj", "b_h"):
        inputs[name] = chunked(inputs[name])
    inputs["b_qk"] = b_qkv[0:2 * D].reshape(2, C, P).transpose(2, 0, 1)
    inputs["b_v"] = b_qkv[2 * D:3 * D]
    arrays = {name: np.ascontiguousarray(a) for name, a in inputs.items()}
    arrays["ident_in"] = np.eye(P, dtype=np.float32)
    arrays["causal_in"] = (np.triu(np.ones((P, P)), 1) * (-10000.0 * ROOT)).astype(np.float32)
    arrays["headmask_in"] = (np.arange(D)[None, :] // DH == np.arange(P)[:, None] % H).astype(np.float32)

    nc = bacc.Bacc("TRN2", target_bir_lowering=False, num_devices=1)
    aps = {name: nc.dram_tensor(name, a.shape, mybir.dt.from_np(a.dtype), kind="ExternalInput").ap()
           for name, a in arrays.items()}
    out = nc.dram_tensor("out", (B, S, D), F32, kind="ExternalOutput").ap()
    attention_recurrence(nc, out=out, **aps)
    return run_bass_kernel_spmd(nc, [arrays], core_ids=[0]).results[0]["out"]
```

```python
from contextlib import ExitStack

import concourse.bass as bass
from concourse import mybir

P = 128
Q = 32
B = 8
S = 512
D = 512
H = 16
DH = D // H
C = D // P
HC = H // C
BLOCKS = S // P
PAIRS = B // 2
UNITS = 2 * H
STEPS = S // (BLOCKS * PAIRS)
HALF = STEPS // 2
SCALE = DH ** -0.5
ROOT = DH ** 0.5
BANK = 512
KEYLAG, PVLAG, HELD = 2, 4, 3

F32 = mybir.dt.float32
F32R = mybir.dt.float32r
ALU = mybir.AluOpType
ACT = mybir.ActivationFunctionType

LEAD = 6
V_STORES = 32 * PAIRS * (BLOCKS - 1)
KQ_STORES = 16 * 6
WEIGHT_LOADS = 16 * 2
SETUP_LOADS = 16 * 11


WAITS = {("xt", 1), ("norm", 1)}


def order(p):
    if p == BLOCKS:
        pieces = []
    else:
        n = p + 1
        pieces = [("xt", e, 0.5) for e in range(2)]
        pieces += [(kind, c, 1.4) for c0 in (0, C // 2) for kind in "qk" for c in (c0, c0 + 1)]
        pieces += [("v", e, 1.4) for e in range(4)] + [("imgscore", e, 1.7) for e in range(2)]
        for u in range(UNITS + PVLAG):
            w = max(0.22, 0.055 * n) * (u < UNITS) + 0.12 * n * (KEYLAG <= u < UNITS + KEYLAG) + 0.1 * n * (u >= PVLAG)
            pieces.append(("head", u, w))
            if u % H == 0 and u:
                pieces.append(("imgprob", u // H - 1, 0.0))
            if u % H == 1 and u > H:
                pieces.append(("imgturn", u // H - 1, 1.0))
            if u % H == PVLAG - 1 and u >= H:
                pieces.append(("norm", u // H - 1, 1.7))
        pieces += [("proj", c, 1.4) for c in range(C)]
    events = []
    total = sum(w for _, _, w in pieces) or 1
    done, step = 0.0, 0

    def steps_until(last):
        nonlocal step
        while step < last:
            events.append(("step", step))
            step += 1
            if step == HALF + 2:
                events.append(("out", 0))

    for kind, i, w in pieces:
        events.append((kind, i))
        done += w
        if p and step < STEPS - 1 and (step < int(STEPS * done / total + 1e-6) or (kind, i) in WAITS):
            steps_until(step + 1)
    if p:
        steps_until(STEPS)
    if p < BLOCKS:
        events += [("wx" if p < BLOCKS - 1 else "keep", c) for c in range(C)] + [("x1n", e) for e in range(2)]
    if p:
        events.append(("out", 1))
    return events


JOBS = ("xt", "q", "k", "v", "imgscore", "proj", "wx", "x1n", "out")


def jobs(p):
    n, out = 0, {}
    for kind, i in order(p):
        for name in ([kind] if kind in JOBS else ["pimgt", "rbc"] if kind == "imgturn" else []):
            out[name, i] = n
            n += 1
    assert n % 2 == 0
    out["count"] = n
    return out


def attention_recurrence(nc, x, cond, mask, w_qkv, b_qk, b_v, w_proj, b_proj, uk_w, uk_b, uv_w, uv_b,
                         w_x, w_h, b_h, ident_in, causal_in, headmask_in, out):
    JOB = [jobs(p) for p in range(BLOCKS + 1)]
    base = [0]
    for p in range(BLOCKS):
        base.append(base[-1] + PAIRS * JOB[p]["count"])

    with ExitStack() as ctx:
        def sb(name, shape, dt=F32):
            return ctx.enter_context(nc.sbuf_tensor(name, shape, dt))

        def sem(name):
            return ctx.enter_context(nc.semaphore(name))

        wqkv_hi = sb("wqkv_hi", [P, C, 3 * D], F32R)
        wqkv_lo = sb("wqkv_lo", [P, C, 3 * D], F32R)
        wproj_hi = sb("wproj_hi", [P, C, D], F32R)
        wproj_lo = sb("wproj_lo", [P, C, D], F32R)
        wx = sb("wx", [P, C, D])
        wh = sb("wh", [P, C, D])
        bqk = sb("bqk", [P, 2, C])
        bv = sb("bv", [P, D])
        bproj = sb("bproj", [P, C])
        bx = sb("bx", [P, C])
        ukb = sb("ukb", [P, C])
        ident = sb("ident", [P, P])
        causal = sb("causal", [P, P])
        xin = sb("xin", [P, 2, D])
        xT_hi = sb("xT_hi", [P, C, 2 * P], F32R)
        xT_lo = sb("xT_lo", [P, C, 2 * P], F32R)
        qT = sb("qT", [P, C, 2 * P])
        qT_hi = sb("qT_hi", [P, C, 2 * P], F32R)
        qT_lo = sb("qT_lo", [P, C, 2 * P], F32R)
        kq = sb("kq", [P, 2, HC, P + S], F32R)
        vst = sb("vst", [P, 2, BLOCKS, D])
        msk = sb("msk", [P, 2, S])
        kimg = sb("kimg", [P, C, B, HC])
        vimg = sb("vimg", [H, 2, D])
        probs = sb("probs", [P, HELD, S])
        probsT = sb("probsT", [P, 2, S])
        nmax = sb("nmax", [P, 2, H])
        nimg = sb("nimg", [P, 2, H])
        rowsum = sb("rowsum", [P, 2, H])
        dimg = sb("dimg", [P, 2, H])
        pimg = sb("pimg", [P, 2, H])
        total = sb("total", [P, 2, H])
        rinv = sb("rinv", [P, 2, H])
        pimgT = sb("pimgT", [H, P])
        attnT_hi = sb("attnT_hi", [P, C, 2 * P], F32R)
        attnT_lo = sb("attnT_lo", [P, C, 2 * P], F32R)
        x1T = sb("x1T", [P, C, 2 * P])
        x1nat = sb("x1nat", [P, 2, D])
        xw = sb("xw", [P, PAIRS, PAIRS, C, 2, STEPS])
        pre = sb("pre", [P, C, Q])
        hist = sb("hist", [P, 2, C, B, HALF])
        x1out = sb("x1out", [P, D])
        osb = sb("osb", [P, D])
        imgT = sb("imgT", [P, C, B])

        dense = [ctx.enter_context(nc.psum_tensor(f"dense{i}", [P, BANK], F32)) for i in range(2)]
        scores = [ctx.enter_context(nc.psum_tensor(f"scores{i}", [P, BANK], F32)) for i in range(2)]
        turned = [ctx.enter_context(nc.psum_tensor(f"turned{i}", [P, BANK], F32)) for i in range(2)]
        pv = ctx.enter_context(nc.psum_tensor("pv", [P, BANK], F32))
        rec = ctx.enter_context(nc.psum_tensor("rec", [P, BANK], F32))

        kT_hi, kT_lo = attnT_hi, attnT_lo
        rinvx = x1nat[:, 0, :].rearrange("p (h q) -> p h q", h=H)
        rbc = x1nat[:, 1, :].rearrange("p (c q) -> p c q", c=C)
        headmask = qT[:, 0:2, :].rearrange("p a n -> p (a n)")
        cond_sb = osb[0:B, :]
        image_w = [wx, wh]
        xw_flat = xw[:].rearrange("p a b c e t -> p (a b c e t)")
        probs_flat = probs[:].rearrange("p a n -> p (a n)")
        W2 = 3 * D // 2
        raw_qkv = [xw_flat[:, W2 * i:W2 * (i + 1)] for i in range(5)]
        raw_qkv += [probs_flat[:, 0:W2], x1T[:].rearrange("p f t -> p (f t)")[:, 0:W2],
                    msk[:].rearrange("p e n -> p (e n)")[:, 0:W2]]
        raw_proj = [vst[:, c // 2, 2 + c % 2, :] for c in range(C)]
        imgTx = rbc.rearrange("p f (b h) -> p f b h", b=B)
        pre_all = pre[:].rearrange("p f q -> p (f q)")
        x1kept = xw[:].rearrange("p a b f e t -> p a b (f e t)").rearrange(
            "p a b (k f e t) -> p a b k f e t", k=2, f=C, e=2)
        x1step = qT[:].rearrange("p f t -> p (f t)").rearrange("p (k f b t) -> p k f b t", k=2, f=C, b=B)

        kq_dram = nc.dram_tensor("kq_dram", [3, PAIRS, P, C, 2, P + S], F32, kind="Internal").ap()
        v_dram = nc.dram_tensor("v_dram", [B, S, D], F32, kind="Internal").ap()
        vimg_dram = nc.dram_tensor("vimg_dram", [B, H, D], F32, kind="Internal").ap()
        x1_dram = nc.dram_tensor("x1_dram", [B, S, D], F32, kind="Internal").ap()

        weights_loaded = sem("weights_loaded")
        qkv_loaded = [sem(f"qkv_loaded{i}") for i in range(2 * C)]
        proj_loaded = sem("proj_loaded")
        bv_loaded = sem("bv_loaded")
        high_ready = sem("high_ready")
        low_ready = sem("low_ready")
        setup_loaded = sem("setup_loaded")
        setup_turned = sem("setup_turned")
        setup_copied = sem("setup_copied")
        setup_product = sem("setup_product")
        zeroed = sem("zeroed")
        image_ready = sem("image_ready")
        kimg_ready = sem("kimg_ready")
        x_loaded = sem("x_loaded")
        staged = [sem(f"staged{e}") for e in range(2)]
        mask_scaled = sem("mask_scaled")
        mask_ready = sem("mask_ready")
        q_high = sem("q_high")
        k_high = sem("k_high")
        q_whole = sem("q_whole")
        tile_loaded = [sem(f"tile_loaded{i}") for i in range(2)]
        dense_ready = sem("dense_ready")
        dense_copied = [sem(f"dense_copied{i}") for i in range(2)]
        scores_ready = sem("scores_ready")
        shifted_ready = sem("shifted_ready")
        probs_ready = sem("probs_ready")
        turned_ready = sem("turned_ready")
        turned_copied = [sem(f"turned_copied{i}") for i in range(2)]
        pv_done = sem("pv_done")
        dimg_ready = sem("dimg_ready")
        pimg_ready = sem("pimg_ready")
        total_ready = sem("total_ready")
        recip_ready = sem("recip_ready")
        rinv_ready = sem("rinv_ready")
        attn_summed = sem("attn_summed")
        attn_ready = sem("attn_ready")
        attn_high = sem("attn_high")
        attn_split = sem("attn_split")
        xT_high = sem("xT_high")
        x1_begun = sem("x1_begun")
        x1_kept = sem("x1_kept")
        x1_set_out = [sem(f"x1_set_out{i}") for i in range(2)]
        kq_stored = [sem(f"kq_stored{i}") for i in range(2)]
        v_stored = sem("v_stored")
        x1_stored = sem("x1_stored")
        x1out_loaded = sem("x1out_loaded")
        rec_ready = sem("rec_ready")
        rec_turned = sem("rec_turned")
        pre_ready = sem("pre_ready")
        h_ready = sem("h_ready")
        out_stored = sem("out_stored")

        def folded(ap):
            return ap.rearrange("p (j f c) -> p f j c", j=C, f=C)

        def trip(p, r):
            return r + PAIRS * p

        def job(p, r, name, i):
            return r * JOB[p]["count"] + (base[p] + JOB[p][name, i])

        def wait_dense(eng, p, r, name, i):
            eng.wait_ge(dense_ready, job(p, r, name, i) + 1)

        def wait_copied(eng, p, r, name, i):
            n = JOB[p][name, i]
            eng.wait_ge(dense_copied[n % 2], since(r * (JOB[p]["count"] // 2) + (base[p] // 2 + n // 2 + 1)))

        def wait_bank(eng, p, r, name, i):
            n = JOB[p][name, i]
            eng.wait_ge(dense_copied[n % 2], since(r * (JOB[p]["count"] // 2) + (base[p] // 2 + n // 2)))

        def bank(p, name, i):
            return dense[JOB[p][name, i] % 2]

        def copied(p, name, i):
            return dense_copied[JOB[p][name, i] % 2]

        def staged_by(p, r):
            return r * 32 + 32 if p == 0 else r * 48 + (PAIRS * 32 + (p - 1) * PAIRS * 48 + 48)

        def step_count(p, r, s):
            return r * STEPS + ((p - 1) * PAIRS * STEPS + s)

        def rec_bank(p, i):
            return scores[0] if p == BLOCKS and i % 2 == 0 else rec

        def split_product(out, hi, lo, moving_hi, moving_lo, first, last):
            pe = nc.tensor
            pe.matmul(out, hi, moving_hi, start=first, stop=False)
            pe.matmul(out, hi, moving_lo, start=False, stop=False)
            return pe.matmul(out, lo, moving_hi, start=False, stop=last)

        def since(n):
            return n + LEAD

        def after_vimg(n):
            return n + 16

        def alone(eng):
            eng.nop(nofuse=True)

        block = ctx.enter_context(nc.Block())

        @block.sync
        def _(sp):
            for tile, a in ((ident[:], ident_in), (cond_sb, cond), (ukb[:], uk_b), (headmask, headmask_in),
                            (bv[:], uv_b.rearrange("(a n) -> a n", a=1).broadcast_to([P, D])),
                            (bqk[:], b_qk), (bproj[:], b_proj), (bx[:], b_h), (causal[:], causal_in),
                            (vst[:, 0, :, :], uk_w), (vst[:, 1, :, :], uv_w)):
                sp.dma_start(tile, a).then_inc(setup_loaded, 16)
            for i in range(2 * C):
                f, half = divmod(i, 2)
                sp.dma_start(raw_qkv[i], w_qkv[:, f, W2 * half:W2 * (half + 1)]).then_inc(qkv_loaded[i], 16)
            sp.wait_ge(setup_turned, 2 * C)
            for c in range(C):
                sp.dma_start(raw_proj[c], w_proj[:, c, :]).then_inc(proj_loaded, 16)
            sp.wait_ge(setup_product, 2)
            for tile, w in ((wx, w_x), (wh, w_h)):
                sp.dma_start(tile[:], w).then_inc(weights_loaded, 16)
            sp.wait_ge(image_ready, 1)
            sp.dma_start(bv[:], b_v.rearrange("(a n) -> a n", a=1).broadcast_to([P, D])).then_inc(bv_loaded, 16)
            for stored in (v_stored, x1_stored, out_stored):
                sp.wait_ge(stored, after_vimg(0))
            sp.wait_ge(low_ready, 2 * C)

            for p in range(BLOCKS):
                with sp.Fori(0, PAIRS) as r:
                    g = trip(p, r)
                    sp.wait_ge(attn_summed, since(g * 2))
                    for e in range(2):
                        sp.dma_start(xin[:, e, :], x[bass.ds(r * 2 + e, 1), P * p:P * p + P, :]).then_inc(x_loaded, 16)
                    sp.wait_ge(v_stored, after_vimg(g * 32) if p < BLOCKS - 1 else after_vimg(V_STORES))
                    for e in range(2):
                        batch = bass.ds(r * 2 + e, 1)
                        sp.dma_start(msk[:, e, 0:P * (p + 1)], mask[batch, 0, 0, 0:P * (p + 1)]
                                     .broadcast_to([P, P * (p + 1)])).then_inc(staged[e], 16)
                        sp.dma_start(vimg[:, e, :], vimg_dram[batch, :, :]).then_inc(staged[e], 16)
                        if p:
                            sp.dma_start(vst[:, e, 0:p, :], v_dram[batch, 0:P * p, :]
                                         .rearrange("a (n q) d -> a q n d", q=P)).then_inc(staged[e], 16)
                    for k in range(2 * C):
                        e, c = divmod(k, C)
                        if k < 2:
                            for name, parts, at in (("q", (qT_hi, qT_hi, qT_lo), 0),
                                                    ("k", (kT_hi, kT_lo, kT_hi), P * (p + 1))):
                                wait_copied(sp, p, r, name, 2 * k)
                                wait_copied(sp, p, r, name, 2 * k + 1)
                                alone(sp)
                                for part, src in enumerate(parts):
                                    sp.dma_start(kq_dram[part, bass.ds(r, 1), :, 2 * k:2 * k + 2, :, at:at + P]
                                                 .rearrange("a q c e t -> q (a c e) t"),
                                                 src[:, 2 * k:2 * k + 2, :].bitcast(F32)
                                                 .rearrange("p c (e t) -> p (c e) t", e=2)).then_inc(kq_stored[k], 16)
                        if k in (0, 2):
                            sp.wait_ge(kq_stored[k // 2], g * KQ_STORES + KQ_STORES)
                            alone(sp)
                        sp.wait_ge(scores_ready, since(g * UNITS + HC * (k - 1)))
                        alone(sp)
                        for part in range(3):
                            sp.dma_start(kq[Q * part:Q * part + Q, k % 2, :, 0:P + P * (p + 1)].bitcast(F32),
                                         kq_dram[part, bass.ds(r, 1), :, c, e, 0:P + P * (p + 1)]
                                         .rearrange("a (j d) t -> d (a j) t", d=Q)).then_inc(tile_loaded[k % 2], 16)

        @block.gpsimd
        def _(pool):
            for lead in [*dense_copied, *turned_copied, shifted_ready, turned_ready, pv_done, attn_summed,
                         attn_ready, scores_ready]:
                pool.sem_inc(lead, LEAD)
            pool.wait_ge(image_ready, 2)
            for rows, stored in ((slice(0, 3 * Q // 2), v_stored), (slice(3 * Q // 2, 3 * Q), x1_stored),
                                 (slice(3 * Q, P), out_stored)):
                pool.dma_start(vimg_dram.rearrange("b h d -> (b h) d")[rows, :], xin[rows, 0, :]).then_inc(stored, 16)
            pool.wait_ge(setup_loaded, SETUP_LOADS)

            def load_x1(p, r, k):
                pool.dma_start(x1out[:], x1_dram[:, bass.ds(r * STEPS + ((p - 1) * P + k * HALF), HALF), :]
                               ).then_inc(x1out_loaded, 16)

            for p in range(BLOCKS + 1):
                if p:
                    pool.wait_ge(x1_stored, after_vimg(p * PAIRS * 32))
                with pool.Fori(0, PAIRS) as r:
                    g = trip(p, r)
                    for kind, i in order(p):
                        if kind == "xt" and i == 0:
                            for e in range(2):
                                pool.wait_ge(staged[e], staged_by(p, r))
                                alone(pool)
                                pool.tensor_scalar(msk[:, e, 0:P * (p + 1)], msk[:, e, 0:P * (p + 1)], ROOT, None,
                                                   ALU.mult).then_inc(mask_scaled, 1)
                                pool.wait_ge(mask_scaled, g * 2 + (e + 1))
                                pool.tensor_tensor(msk[:, e, P * p:P * (p + 1)], msk[:, e, P * p:P * (p + 1)],
                                                   causal[:], ALU.add).then_inc(mask_ready, 1)
                        elif kind == "k" and i == C // 2:
                            wait_copied(pool, p, r, "q", C - 2)
                            wait_copied(pool, p, r, "q", C - 1)
                            alone(pool)
                            pool.tensor_tensor(qT[:], qT_hi[:].bitcast(F32), qT_lo[:].bitcast(F32), ALU.add).then_inc(q_whole, 1)
                        elif kind == "head" and i == 2 and p < BLOCKS - 1:
                            for e in range(2):
                                wait_copied(pool, p, r, "v", 2 + e)
                            alone(pool)
                            for e in range(2):
                                pool.dma_start(v_dram[bass.ds(r * 2 + e, 1), P * p:P * p + P, :],
                                               vst[:, e, p, :]).then_inc(v_stored, 16)
                        elif kind == "x1n":
                            wait_copied(pool, p, r, "x1n", i)
                            alone(pool)
                            pool.dma_start(x1_dram[bass.ds(r * 2 + i, 1), P * p:P * p + P, :],
                                           x1nat[:, i, :]).then_inc(x1_stored, 16)
                        elif kind == "step" and i == 0:
                            load_x1(p, r, 0)
                        elif kind == "out":
                            wait_copied(pool, p, r, "out", i)
                            alone(pool)
                            pool.dma_start(out[:, bass.ds(r * STEPS + ((p - 1) * P + i * HALF), HALF), :], osb[:]
                                           ).then_inc(out_stored, 16)
                            if i == 0:
                                load_x1(p, r, 1)
            pool.wait_ge(out_stored, after_vimg(16 * 2 * PAIRS * BLOCKS))
            pool.wait_ge(v_stored, after_vimg(V_STORES))
            pool.wait_ge(x1_stored, after_vimg(32 * PAIRS * BLOCKS))

        @block.scalar
        def _(act):
            for i in range(2 * C):
                f, half = divmod(i, 2)
                act.wait_ge(qkv_loaded[i], 16)
                act.copy(wqkv_hi[:, f, W2 * half:W2 * (half + 1)], raw_qkv[i]).then_inc(high_ready, 1)
            act.wait_ge(setup_loaded, SETUP_LOADS)
            act.wait_ge(proj_loaded, 16 * C)
            for c in range(C):
                act.copy(wproj_hi[:, c, :], raw_proj[c]).then_inc(high_ready, 1)
            for p in range(BLOCKS + 1):
                n = P * (p + 1)

                def head(r, u):
                    g = trip(p, r)
                    v = u - KEYLAG
                    if 0 <= v < UNITS and v % 2:
                        act.wait_ge(turned_ready, since(g * UNITS + (v + 1)))
                        act.wait_ge(pv_done, since(g * UNITS + (v - 1)))
                        act.copy(probsT[:, 1, 0:n], turned[1][:, 0:n]).then_inc(turned_copied[1], 1)
                    if u < UNITS:
                        e, h = divmod(u, H)
                        act.wait_ge(shifted_ready, since(g * UNITS + (u + 1)))
                        act.activation(probs[:, u % HELD, 0:n], probs[:, u % HELD, 0:n], ACT.Exp, scale=-1.0,
                                       bias=nmax[:, e, h:h + 1], accum_out=rowsum[:, e, h:h + 1]).then_inc(probs_ready, 1)

                with act.Fori(0, PAIRS) as r:
                    g = trip(p, r)
                    for kind, i in order(p):
                        if kind == "xt":
                            wait_dense(act, p, r, "xt", i)
                            act.copy(xT_hi[:, :, P * i:P * i + P],
                                     bank(p, kind, i)[:, :].rearrange("p (f t) -> p f t", f=C)).then_inc(xT_high, 1)
                        elif kind == "q":
                            wait_dense(act, p, r, "q", i)
                            act.activation(qT_hi[:, i, :], bank(p, kind, i)[:, 0:2 * P], ACT.Identity,
                                           bias=bqk[:, 0, i:i + 1]).then_inc(q_high, 1)
                        elif kind == "k":
                            wait_dense(act, p, r, "k", i)
                            act.activation(kT_hi[:, i, :], bank(p, kind, i)[:, 0:2 * P], ACT.Identity,
                                           bias=bqk[:, 1, i:i + 1]).then_inc(k_high, 1)
                        elif kind == "head":
                            head(r, i)
                        elif kind == "imgprob":
                            act.wait_ge(dimg_ready, g * 2 + (i + 1))
                            act.activation(pimg[:, i, :], dimg[:, i, :], ACT.Exp).then_inc(pimg_ready, 1)
                        elif kind == "imgturn":
                            wait_dense(act, p, r, "pimgt", i)
                            act.copy(pimgT[:], bank(p, "pimgt", i)[0:H, 0:P]).then_inc(copied(p, "pimgt", i), 1)
                            wait_dense(act, p, r, "rbc", i)
                            act.copy(x1nat[:, 1, :], bank(p, "rbc", i)[:, :]
                                     ).then_inc(copied(p, "rbc", i), 1)
                        elif kind == "norm":
                            for stored in kq_stored:
                                act.wait_ge(stored, g * KQ_STORES + KQ_STORES)
                            act.wait_ge(attn_ready, since(g * 2 + (i + 1)))
                            act.copy(attnT_hi[:, :, P * i:P * i + P], x1T[:, :, P * i:P * i + P]).then_inc(attn_high, 1)
                        elif kind == "wx":
                            wait_dense(act, p, r, "wx", i)
                            cells = xw[:, bass.ds(r, 1), :, i] if p % 2 == 0 else xw[:, :, bass.ds(r, 1), i]
                            act.activation(cells.rearrange("p a g e t -> p (a g) e t"),
                                           bank(p, kind, i)[:, 0:2 * P].rearrange("p (e g t) -> p g e t", e=2, g=PAIRS),
                                           ACT.Identity, bias=bx[:, i:i + 1]).then_inc(copied(p, kind, i), 1)
                        elif kind == "keep":
                            wait_copied(act, p, r, "proj", i)
                            alone(act)
                            act.copy(x1kept[:, :, bass.ds(r, 1), :, i, :, :].rearrange("p a b k e t -> p (a b) k e t"),
                                     x1T[:, i, :].rearrange("p (e a k t) -> p a k e t", e=2, a=PAIRS, k=2)
                                     ).then_inc(x1_kept, 1)
                        elif kind == "x1n":
                            wait_dense(act, p, r, "x1n", i)
                            act.copy(folded(x1nat[:, i, :]),
                                     bank(p, kind, i)[:, :].rearrange("p (f j c) -> p f j c", f=C, j=C)
                                     ).then_inc(copied(p, kind, i), 1)
                        elif kind == "step":
                            act.wait_ge(pre_ready, step_count(p, r, i) + 1)
                            act.activation(hist[:, i // HALF, :, :, i % HALF], pre[:, :, 0:B], ACT.Tanh).then_inc(h_ready, 1)

        @block.vector
        def _(dve):
            dve.memset(rec[:], 0.0).then_inc(zeroed, 1)
            dve.memset(kimg[:], 0.0).then_inc(zeroed, 1)
            dve.wait_ge(zeroed, 2)
            for e, banks in ((0, scores + turned), (1, dense + [pv, scores[1]])):
                for f in range(C):
                    dve.wait_ge(setup_turned, e * C + f + 1)
                    dve.tensor_copy(image_w[e][:, f, :], banks[f][:, :]).then_inc(setup_copied, 1)
            dve.wait_ge(setup_turned, 2 * C + 1)
            dve.tensor_copy(imgT[:], scores[0][:, 0:C * B].rearrange("p (f b) -> p f b", f=C)).then_inc(setup_copied, 1)
            dve.tensor_copy(hist[:, 1, :, :, HALF - 1],
                            scores[0][:, 0:C * B].rearrange("p (f b) -> p f b", f=C)).then_inc(h_ready, 1)
            dve.wait_ge(setup_copied, 2 * C + 1)
            dve.tensor_copy(imgTx, imgT[:].unsqueeze(3).broadcast_to([P, C, B, H])).then_inc(setup_copied, 1)
            dve.wait_ge(setup_product, 1)
            for j in range(HC):
                rows = slice(Q * j, Q * j + Q)
                dve.tensor_tensor(kimg[rows, :, :, j], scores[1][rows, 0:C * B].rearrange("p (c b) -> p c b", c=C),
                                  ukb[rows, :].unsqueeze(2).broadcast_to([Q, C, B]), ALU.add).then_inc(kimg_ready, 1)
            dve.wait_ge(setup_product, 2)
            dve.tensor_tensor(xin[:, 1, :], turned[0][:, :], bv[:], ALU.add).then_inc(image_ready, 1)
            dve.wait_ge(image_ready, 1)
            dve.tensor_tensor(xin[:, 0, :], xin[:, 1, :], headmask, ALU.mult).then_inc(image_ready, 1)
            for i in range(2 * C):
                f, half = divmod(i, 2)
                part = slice(W2 * half, W2 * (half + 1))
                dve.wait_ge(high_ready, i + 1)
                dve.tensor_tensor(wqkv_lo[:, f, part], raw_qkv[i], wqkv_hi[:, f, part].bitcast(F32), ALU.subtract
                                  ).then_inc(low_ready, 1)
            for c in range(C):
                dve.wait_ge(high_ready, 2 * C + c + 1)
                dve.tensor_tensor(wproj_lo[:, c, :], raw_proj[c], wproj_hi[:, c, :].bitcast(F32), ALU.subtract
                                  ).then_inc(low_ready, 1)

            for p in range(BLOCKS + 1):
                n = P * (p + 1)
                if p == BLOCKS:
                    dve.wait_ge(x1_kept, C * PAIRS)
                elif p:
                    for i in range(2):
                        dve.wait_ge(dense_copied[i], since(base[p] // 2))

                def head(r, u):
                    g = trip(p, r)
                    if u < UNITS:
                        e, h = divmod(u, H)
                        dve.wait_ge(scores_ready, since(g * UNITS + (u + 1)))
                        dve.wait_ge(turned_ready, since(g * UNITS + (u - HELD + 1)))
                        if h == 0:
                            dve.wait_ge(mask_ready, g * 2 + (e + 1))
                        alone(dve)
                        dve.tensor_tensor_reduce(out=probs[:, u % HELD, 0:n], in0=scores[u % 2][:, 0:n],
                                                 in1=msk[:, e, 0:n], scale=-SCALE, scalar=nimg[:, e, h:h + 1],
                                                 op0=ALU.add, op1=ALU.min, accum_out=nmax[:, e, h:h + 1]
                                                 ).then_inc(shifted_ready, 1)
                    v = u - KEYLAG
                    if 0 <= v < UNITS and v % 2 == 0:
                        dve.wait_ge(turned_ready, since(g * UNITS + (v + 1)))
                        dve.wait_ge(pv_done, since(g * UNITS + (v - 1)))
                        dve.tensor_copy(probsT[:, 0, 0:n], turned[0][:, 0:n]).then_inc(turned_copied[0], 1)

                def set_out(r, half):
                    alone(dve)
                    dve.tensor_copy(x1step[:, half].rearrange("p f b t -> p f (b t)")
                                    .rearrange("p f (g u) -> p g f u", g=PAIRS),
                                    x1kept[:, bass.ds(r, 1), :, half].rearrange("p a g f e t -> p (a g) f (e t)")
                                    ).then_inc(x1_set_out[half], 1)

                with dve.Fori(0, PAIRS) as r:
                    g = trip(p, r)
                    for kind, i in order(p):
                        if kind == "xt":
                            dve.wait_ge(xT_high, g * 2 + (i + 1))
                            dve.tensor_tensor(xT_lo[:, :, P * i:P * i + P],
                                              bank(p, kind, i)[:, :].rearrange("p (f t) -> p f t", f=C),
                                              xT_hi[:, :, P * i:P * i + P].bitcast(F32), ALU.subtract
                                              ).then_inc(copied(p, kind, i), 1)
                        if kind in ("q", "k"):
                            high, hi, lo = (q_high, qT_hi, qT_lo) if kind == "q" else (k_high, kT_hi, kT_lo)
                            t = int(kind == "k")
                            dve.wait_ge(high, g * C + (i + 1))
                            dve.scalar_tensor_tensor(out=lo[:, i, :], in0=bank(p, kind, i)[:, 0:2 * P],
                                                     scalar=bqk[:, t, i:i + 1], in1=hi[:, i, :].bitcast(F32),
                                                     op0=ALU.add, op1=ALU.subtract).then_inc(copied(p, kind, i), 1)
                        elif kind == "v":
                            wait_dense(dve, p, r, "v", i)
                            if i == 0:
                                dve.wait_ge(v_stored, after_vimg(g * 32) if p < BLOCKS - 1 else after_vimg(V_STORES))
                                dve.wait_ge(bv_loaded, 16)
                            e, half = divmod(i, 2)
                            cols = slice(half * D // 2, (half + 1) * D // 2)
                            dve.tensor_tensor(vst[:, e, p, cols], bank(p, kind, i)[:, 0:D // 2], bv[:, cols], ALU.add
                                              ).then_inc(copied(p, kind, i), 1)
                        elif kind == "imgscore":
                            wait_dense(dve, p, r, "imgscore", i)
                            dve.tensor_scalar(nimg[:, i, :], bank(p, kind, i)[:, 0:H], -SCALE, None, ALU.mult
                                              ).then_inc(copied(p, kind, i), 1)
                            wait_copied(dve, p, r, "imgscore", i)
                        elif kind == "head":
                            head(r, i)
                        elif kind == "imgprob":
                            dve.wait_ge(shifted_ready, since(g * UNITS + (i + 1) * H))
                            dve.tensor_tensor(dimg[:, i, :], nmax[:, i, :], nimg[:, i, :], ALU.subtract
                                              ).then_inc(dimg_ready, 1)
                        elif kind == "imgturn":
                            dve.wait_ge(pimg_ready, g * 2 + (i + 1))
                            dve.wait_ge(probs_ready, g * UNITS + (i + 1) * H)
                            dve.tensor_tensor(total[:, i, :], rowsum[:, i, :], pimg[:, i, :], ALU.add
                                              ).then_inc(total_ready, 1)
                            dve.wait_ge(total_ready, g * 2 + (i + 1))
                            dve.reciprocal(rinv[:, i, :], total[:, i, :]).then_inc(recip_ready, 1)
                            dve.wait_ge(recip_ready, g * 2 + (i + 1))
                            dve.wait_ge(x1_stored, after_vimg(g * 32))
                            dve.tensor_copy(rinvx, rinv[:, i, :].unsqueeze(2).broadcast_to([P, H, Q])
                                            ).then_inc(rinv_ready, 1)
                        elif kind == "norm":
                            dve.wait_ge(attn_summed, since(g * 2 + (i + 1)))
                            wait_copied(dve, p, r, "rbc", i)
                            mine = slice(P * i, P * i + P)
                            dve.tensor_tensor(x1T[:, :, mine], pv[:, :].rearrange("p (c q) -> p c q", c=C),
                                              rbc, ALU.mult).then_inc(attn_ready, 1)
                            dve.wait_ge(attn_high, g * 2 + (i + 1))
                            dve.tensor_tensor(attnT_lo[:, :, mine], x1T[:, :, mine], attnT_hi[:, :, mine].bitcast(F32),
                                              ALU.subtract).then_inc(attn_split, 1)
                        elif kind == "proj":
                            wait_dense(dve, p, r, "proj", i)
                            dve.scalar_tensor_tensor(out=x1T[:, i, :], in0=bank(p, kind, i)[:, 0:2 * P],
                                                     scalar=bproj[:, i:i + 1], in1=xT_hi[:, i, :].bitcast(F32),
                                                     op0=ALU.add, op1=ALU.add).then_inc(x1_begun, 1)
                            dve.wait_ge(x1_begun, g * C + (i + 1))
                            dve.tensor_tensor(x1T[:, i, :], x1T[:, i, :], xT_lo[:, i, :].bitcast(F32), ALU.add
                                              ).then_inc(copied(p, kind, i), 1)
                        elif kind == "step":
                            t = step_count(p, r, i)
                            if p == BLOCKS and i == 0:
                                set_out(r, 0)
                            dve.wait_ge(rec_ready, t + 1)
                            dve.transpose(pre_all, rec_bank(p, i)[:, 0:P]).then_inc(rec_turned, 1)
                            dve.wait_ge(rec_turned, t + 1)
                            if p == BLOCKS:
                                dve.tensor_tensor(pre[:, :, 0:B], pre[:, :, 0:B],
                                                  bx[:].unsqueeze(2).broadcast_to([P, C, B]), ALU.add).then_inc(pre_ready, 1)
                                if i == 0:
                                    set_out(r, 1)
                            else:
                                cells = xw[:, :, bass.ds(r, 1), :, :, i] if p % 2 else xw[:, bass.ds(r, 1), :, :, :, i]
                                sums = pre[:, :, 0:B].rearrange("p f (b e) -> p f b e", e=2)
                                dve.tensor_tensor(sums, sums, cells.rearrange("p a g f e -> p f (a g) e"),
                                                  ALU.add).then_inc(pre_ready, 1)
                        elif kind == "out":
                            o = r * 2 + ((p - 1) * PAIRS * 2 + i)
                            wait_dense(dve, p, r, "out", i)
                            dve.wait_ge(x1out_loaded, o * 16 + 16)
                            dve.wait_ge(out_stored, after_vimg(o * 16))
                            dve.tensor_tensor(folded(osb[:]),
                                              bank(p, kind, i)[:, :].rearrange("p (f j c) -> p f j c", f=C, j=C),
                                              folded(x1out[:]), ALU.add).then_inc(copied(p, kind, i), 1)

        @block.tensor
        def _(pe):
            pe.wait_ge(setup_loaded, SETUP_LOADS)
            for e, banks in ((0, scores + turned), (1, dense + [pv, scores[1]])):
                for f in range(C):
                    if (e, f) == (1, C - 1):
                        pe.wait_ge(setup_copied, 2)
                    for o in range(C):
                        last = pe.transpose(banks[f][:, P * o:P * o + P], vst[:, e, o, P * f:P * f + P], ident[:])
                    last.then_inc(setup_turned, 1)
            pe.wait_ge(setup_copied, 2 * C)
            for f in range(C):
                last = pe.transpose(scores[0][:, B * f:B * f + B], cond_sb[:, P * f:P * f + P], ident[0:B, 0:B])
            last.then_inc(setup_turned, 1)
            pe.wait_ge(setup_copied, 2 * C + 1)
            for c in range(C):
                for f in range(C):
                    last = pe.matmul(scores[1][:, B * c:B * c + B], image_w[0][:, f, P * c:P * c + P], imgT[:, f, :],
                                     start=f == 0, stop=f == C - 1)
            last.then_inc(setup_product, 1)
            pe.wait_ge(setup_copied, 2 * C + 2)
            for f in range(C):
                last = pe.matmul(turned[0][:, :], rbc[:, f, :], image_w[1][:, f, :],
                                 start=f == 0, stop=f == C - 1)
            last.then_inc(setup_product, 1)
            pe.wait_ge(image_ready, 2)
            pe.wait_ge(kimg_ready, HC)
            pe.wait_ge(h_ready, 1)
            pe.wait_ge(zeroed, 2)
            pe.wait_ge(low_ready, 2 * C)

            for p in range(BLOCKS + 1):
                n = P * (p + 1)

                def head(r, u):
                    g = trip(p, r)
                    if u < UNITS:
                        e, h = divmod(u, H)
                        c, j = divmod(h, HC)
                        if h == 0:
                            pe.wait_ge(staged[e], staged_by(p, r))
                        k = C * e + c
                        if j == 0:
                            pe.wait_ge(tile_loaded[k % 2], g * (C * 3 * 16) + (k // 2 + 1) * 3 * 16)
                        pe.wait_ge(shifted_ready, since(g * UNITS + (u - 1)))
                        pe.matmul(scores[u % 2][:, 0:n], kq[0:3 * Q, k % 2, j, 0:P],
                                  kq[0:3 * Q, k % 2, j, P:P + n], start=True, stop=True
                                  ).then_inc(scores_ready, 1)
                    if KEYLAG <= u < UNITS + KEYLAG:
                        v = u - KEYLAG
                        pe.wait_ge(probs_ready, g * UNITS + (v + 1))
                        pe.wait_ge(turned_copied[v % 2], since(g * H + (v // 2)))
                        for k in range(p + 1):
                            last = pe.transpose(turned[v % 2][:, P * k:P * k + P], probs[:, v % HELD, P * k:P * k + P], ident[:])
                        last.then_inc(turned_ready, 1)
                    if u >= PVLAG:
                        v = u - PVLAG
                        e, h = divmod(v, H)
                        c, j = divmod(h, HC)
                        pe.wait_ge(turned_copied[v % 2], since(g * H + (v // 2 + 1)))
                        if h == 0:
                            pe.wait_ge(attn_ready, since(g * 2 + e))
                        for k in range(p + 1):
                            last = pe.matmul(pv[Q * j:Q * j + Q, P * c:P * c + P], vst[:, e, k, DH * h:DH * h + DH],
                                             probsT[:, v % 2, P * k:P * k + P], start=c == 0 and k == 0, stop=False,
                                             skip_group_check=True)
                        last.then_inc(pv_done, 1)

                with pe.Fori(0, PAIRS) as r:
                    g = trip(p, r)
                    for kind, i in order(p):
                        if kind in JOBS and kind != "out":
                            wait_bank(pe, p, r, kind, i)
                            d = bank(p, kind, i)
                        if kind == "xt":
                            pe.wait_ge(x_loaded, g * 32 + 32)
                            for f in range(C):
                                last = pe.transpose(d[:, P * f:P * f + P], xin[:, i, P * f:P * f + P], ident[:])
                            last.then_inc(dense_ready, 1)
                        elif kind in ("q", "k"):
                            if kind == "q" and i == 0:
                                wait_copied(pe, p, r, "xt", 0)
                                wait_copied(pe, p, r, "xt", 1)
                            w0 = D * (kind == "k") + P * i
                            for f in range(C):
                                last = split_product(d[:, 0:2 * P], wqkv_hi[:, f, w0:w0 + P], wqkv_lo[:, f, w0:w0 + P],
                                                     xT_hi[:, f, :], xT_lo[:, f, :], f == 0, f == C - 1)
                            last.then_inc(dense_ready, 1)
                        elif kind == "v":
                            e, half = divmod(i, 2)
                            w0 = 2 * D + half * D // 2
                            for f in range(C):
                                last = split_product(d[:, 0:D // 2], xT_hi[:, f, P * e:P * e + P], xT_lo[:, f, P * e:P * e + P],
                                                     wqkv_hi[:, f, w0:w0 + D // 2], wqkv_lo[:, f, w0:w0 + D // 2],
                                                     f == 0, f == C - 1)
                            last.then_inc(dense_ready, 1)
                        elif kind == "imgscore":
                            pe.wait_ge(q_whole, g + 1)
                            for c in range(C):
                                last = pe.matmul(d[:, HC * c:HC * c + HC], qT[:, c, P * i:P * i + P],
                                                 kimg[:, c, bass.ds(r * 2 + i, 1), :], start=True, stop=True)
                            last.then_inc(dense_ready, 1)
                        elif kind == "head":
                            head(r, i)
                        elif kind == "imgturn":
                            pe.wait_ge(pimg_ready, g * 2 + (i + 1))
                            wait_bank(pe, p, r, "pimgt", i)
                            pe.transpose(bank(p, "pimgt", i)[0:H, 0:P], pimg[:, i, :], ident[:]).then_inc(dense_ready, 1)
                            pe.wait_ge(rinv_ready, g * 2 + (i + 1))
                            wait_bank(pe, p, r, "rbc", i)
                            for c in range(C):
                                last = pe.transpose(bank(p, "rbc", i)[:, P * c:P * c + P],
                                                    rinvx[:, HC * c:HC * c + HC, :].rearrange("p j q -> p (j q)"),
                                                    ident[:])
                            last.then_inc(dense_ready, 1)
                        elif kind == "norm":
                            wait_copied(pe, p, r, "pimgt", i)
                            for c in range(C):
                                last = pe.matmul(pv[:, P * c:P * c + P], vimg[:, i, P * c:P * c + P], pimgT[:],
                                                 start=False, stop=True, skip_group_check=True)
                            last.then_inc(attn_summed, 1)
                        elif kind == "proj":
                            if i == 0:
                                pe.wait_ge(attn_split, g * 2 + 2)
                                pe.wait_ge(low_ready, 3 * C)
                            for c in range(C):
                                last = split_product(d[:, 0:2 * P], wproj_hi[:, c, P * i:P * i + P],
                                                     wproj_lo[:, c, P * i:P * i + P], attnT_hi[:, c, :],
                                                     attnT_lo[:, c, :], c == 0, c == C - 1)
                            last.then_inc(dense_ready, 1)
                        elif kind == "wx":
                            if i == 0:
                                pe.wait_ge(weights_loaded, WEIGHT_LOADS)
                                wait_copied(pe, p, r, "proj", C - 2)
                                wait_copied(pe, p, r, "proj", C - 1)
                            for f in range(C):
                                last = pe.matmul(d[:, 0:2 * P], wx[:, f, P * i:P * i + P], x1T[:, f, :],
                                                 start=f == 0, stop=f == C - 1)
                            last.then_inc(dense_ready, 1)
                        elif kind == "x1n":
                            if i == 0 and p == BLOCKS - 1:
                                wait_copied(pe, p, r, "proj", C - 2)
                                wait_copied(pe, p, r, "proj", C - 1)
                            for f in range(C):
                                last = pe.transpose(d[:, P * f:P * f + P], x1T[:, f, P * i:P * i + P], ident[:])
                            last.then_inc(dense_ready, 1)
                        elif kind == "step":
                            before = (i - 1) % STEPS
                            d = rec_bank(p, i)
                            if p == BLOCKS:
                                if i % HALF == 0:
                                    pe.wait_ge(x1_set_out[i // HALF], r + 1)
                                pe.wait_ge(rec_turned, step_count(p, r, i) - 1)
                                for f in range(C):
                                    for j in range(C):
                                        pe.matmul(d[Q * j:Q * j + B, 0:P], x1step[:, i // HALF, f, :, i % HALF],
                                                  wx[:, f, :].rearrange("p (a j c) -> p a j c", a=C, j=C)[:, :, j, :],
                                                  start=f == 0, stop=False)
                            pe.wait_ge(h_ready, step_count(p, r, i) + 1)
                            for f in range(C):
                                for j in range(C):
                                    last = pe.matmul(d[Q * j:Q * j + B, 0:P], hist[:, before // HALF, f, :, before % HALF],
                                                     wh[:, f, P * j:P * j + P], start=f == 0 and p < BLOCKS,
                                                     stop=f == C - 1)
                            last.then_inc(rec_ready, 1)
                        elif kind == "out":
                            wait_bank(pe, p, r, "out", i)
                            pe.wait_ge(h_ready, r * STEPS + ((p - 1) * PAIRS * STEPS + (i + 1) * HALF + 1))
                            for f in range(C):
                                last = pe.transpose(bank(p, kind, i)[:, P * f:P * f + P],
                                                    hist[:, i, f, :, :].rearrange("p b s -> p (b s)"), ident[:])
                            last.then_inc(dense_ready, 1)


def kernel(x, cond_1024, mask_Bx1x1xS_ff0, L0_cond_c_attn_w, L0_cond_c_attn_b, L0_cond_c_proj_w,
           L0_cond_c_proj_b, L0_cond_uk_w, L0_cond_uk_b, L0_cond_uv_w, L0_cond_uv_b, L1_cond_Wx,
           L1_cond_Wh, L1_cond_b):
    import numpy as np
    import concourse.bacc as bacc
    from concourse.bass_utils import run_bass_kernel_spmd

    inputs = {
        "x": x, "cond": cond_1024, "mask": mask_Bx1x1xS_ff0, "w_qkv": L0_cond_c_attn_w,
        "w_proj": L0_cond_c_proj_w, "b_proj": L0_cond_c_proj_b,
        "uk_w": L0_cond_uk_w, "uk_b": L0_cond_uk_b, "uv_w": L0_cond_uv_w, "uv_b": L0_cond_uv_b,
        "w_x": L1_cond_Wx, "w_h": L1_cond_Wh, "b_h": L1_cond_b,
    }
    b_qkv = L0_cond_c_attn_b

    def folded(a, axis):
        axis %= a.ndim
        cut = a.reshape(a.shape[:axis] + (C, C, Q) + a.shape[axis + 1:])
        return np.swapaxes(cut, axis, axis + 1).reshape(a.shape)

    def chunked(a):
        return np.swapaxes(a.reshape((C, P) + a.shape[1:]), 0, 1)

    inputs["x"] = folded(x, -1)
    inputs["cond"] = folded(cond_1024, -1)
    for name in ("w_qkv", "w_x", "w_h", "b_proj", "b_h"):
        inputs[name] = folded(inputs[name], 0)
    for name in ("w_proj", "w_x", "uk_w", "uv_w"):
        inputs[name] = folded(inputs[name], 1)
    for name in ("w_qkv", "w_proj", "w_x", "w_h", "uk_w", "uv_w", "uk_b", "b_proj", "b_h"):
        inputs[name] = chunked(inputs[name])
    inputs["b_qk"] = b_qkv[0:2 * D].reshape(2, C, P).transpose(2, 0, 1)
    inputs["b_v"] = b_qkv[2 * D:3 * D]
    arrays = {name: np.ascontiguousarray(a) for name, a in inputs.items()}
    arrays["ident_in"] = np.eye(P, dtype=np.float32)
    arrays["causal_in"] = (np.triu(np.ones((P, P)), 1) * (-10000.0 * ROOT)).astype(np.float32)
    arrays["headmask_in"] = (np.arange(D)[None, :] // DH == np.arange(P)[:, None] % H).astype(np.float32)

    nc = bacc.Bacc("TRN2", target_bir_lowering=False, num_devices=1)
    aps = {name: nc.dram_tensor(name, a.shape, mybir.dt.from_np(a.dtype), kind="ExternalInput").ap()
           for name, a in arrays.items()}
    out = nc.dram_tensor("out", (B, S, D), F32, kind="ExternalOutput").ap()
    attention_recurrence(nc, out=out, **aps)
    return run_bass_kernel_spmd(nc, [arrays], core_ids=[0]).results[0]["out"]
```

```python
from contextlib import ExitStack

import concourse.bass as bass
from concourse import mybir

P = 128
Q = 32
B = 8
S = 512
D = 512
H = 16
DH = D // H
C = D // P
HC = H // C
BLOCKS = S // P
PAIRS = B // 2
UNITS = 2 * H
STEPS = S // (BLOCKS * PAIRS)
HALF = STEPS // 2
SCALE = DH ** -0.5
ROOT = DH ** 0.5
BANK = 512
KEYLAG = [4, 2, 2, 2]
PVLAG = [6, 4, 4, 4]
HELD_COLUMNS = 4 * S
HELD = [HELD_COLUMNS // (P * (p + 1)) for p in range(BLOCKS)]
TILES = [2 * (P + S) // (P * (p + 2)) for p in range(BLOCKS)]

F32 = mybir.dt.float32
F32R = mybir.dt.float32r
ALU = mybir.AluOpType
ACT = mybir.ActivationFunctionType

LEAD = 16
V_STORES = 32 * PAIRS * (BLOCKS - 1)
KQ_STORES = 16 * 6
WEIGHT_LOADS = 16 * 2
SETUP_LOADS = 16 * 11

WAITS = {("xsplit", 1), ("head", 1), ("head", 18), ("head", 34), ("norm", 1)}


def order(p):
    if p == BLOCKS:
        pieces = []
    else:
        n = p + 1
        pieces = [("xsplit", k, 0.0) for k in range(2)]
        pieces += [(kind, c, 1.25) for c0 in (0, C // 2) for kind in "qk" for c in (c0, c0 + 1)]
        pieces += [("v", e, 1.25) for e in range(4)] + [("imgscore", e, 0.9) for e in range(2)]
        for u in range(UNITS + PVLAG[p]):
            w = max(0.22, 0.055 * n) * (u < UNITS) + 0.1 * n * (u >= PVLAG[p])
            w += 0.12 * n * (KEYLAG[p] <= u < UNITS + KEYLAG[p])
            pieces.append(("head", u, w))
            if u % H == 0 and u:
                pieces.append(("imgprob", u // H - 1, 0.0))
            if u % H == 1 and u > H:
                pieces.append(("imgturn", u // H - 1, 0.2))
            if u % H == 2 and u > H:
                pieces.append(("rowturn", u // H - 1, 0.8))
            if u in (H + PVLAG[p] - 1, UNITS + PVLAG[p] - 1):
                pieces.append(("norm", u // H - 1, 1.1))
        pieces += [("proj", c, 1.4) for c in range(C)]
    events = []
    total = sum(w for _, _, w in pieces) or 1
    done, step = 0.0, 0

    def steps_until(last):
        nonlocal step
        while step < last:
            events.append(("step", step))
            step += 1
            if step == HALF + 2:
                events.append(("out", 0))

    for kind, i, w in pieces:
        events.append((kind, i))
        done += w
        if p and step < STEPS - 1 and (step < int(STEPS * done / total + 1e-6) or (kind, i) in WAITS):
            steps_until(step + 1)
    if p:
        steps_until(STEPS)
    if p < BLOCKS:
        x1_products = [("wx" if p < BLOCKS - 1 else "keep", c) for c in range(C)]
        x1_rows = [("x1n", e) for e in range(2)]
        events += x1_products + x1_rows if p < BLOCKS - 1 else x1_rows + x1_products
    if p:
        events.append(("out", 1))
    return events


SIDE_JOBS = {"imgturn": "pimgt", "rowturn": "rbc"}
JOBS = ("q", "k", "v", "imgscore", "proj", "wx", "x1n", "out")


def jobs(p):
    n, out = 0, {}
    for kind, i in order(p):
        for name in ([kind] if kind in JOBS else [SIDE_JOBS[kind]] if kind in SIDE_JOBS else []):
            out[name, i] = n
            n += 1
    assert n % 2 == 0
    out["count"] = n
    return out


def attention_recurrence(nc, x, cond, mask, w_qkv, b_qk, b_v, w_proj, b_proj, uk_w, uk_b, uv_w, uv_b,
                         w_x, w_h, b_h, ident_in, causal_in, headmask_in, out):
    JOB = [jobs(p) for p in range(BLOCKS + 1)]
    base = [0]
    for p in range(BLOCKS):
        base.append(base[-1] + PAIRS * JOB[p]["count"])

    with ExitStack() as ctx:
        def sb(name, shape, dt=F32):
            return ctx.enter_context(nc.sbuf_tensor(name, shape, dt))

        def sem(name):
            return ctx.enter_context(nc.semaphore(name))

        wqkv_hi = sb("wqkv_hi", [P, C, 3 * D], F32R)
        wqkv_lo = sb("wqkv_lo", [P, C, 3 * D], F32R)
        wproj_hi = sb("wproj_hi", [P, C, D], F32R)
        wproj_lo = sb("wproj_lo", [P, C, D], F32R)
        wx = sb("wx", [P, C, D])
        wh = sb("wh", [P, C, D])
        bqk = sb("bqk", [P, 2, C])
        bv = sb("bv", [P, D])
        bproj = sb("bproj", [P, C])
        bx = sb("bx", [P, C])
        ukb = sb("ukb", [P, C])
        ident = sb("ident", [P, P])
        causal = sb("causal", [P, P])
        xin = sb("xin", [P, C, 2 * P])
        xT_hi = sb("xT_hi", [P, C, 2 * P], F32R)
        xT_lo = sb("xT_lo", [P, C, 2 * P], F32R)
        qT = sb("qT", [P, C, 2 * P])
        qT_hi = sb("qT_hi", [P, C, 2 * P], F32R)
        qT_lo = sb("qT_lo", [P, C, 2 * P], F32R)
        kq_tiles = sb("kq", [P, 2 * HC * (P + S)], F32R)
        vst = sb("vst", [P, 2, BLOCKS, D])
        msk = sb("msk", [P, 2, S])
        kimg = sb("kimg", [P, C, B, HC])
        vimg = sb("vimg", [H, 2, D])
        probs_held = sb("probs", [P, HELD_COLUMNS])
        probsT = sb("probsT", [P, 2, S])
        nmax = sb("nmax", [P, 2, H])
        nimg = sb("nimg", [P, 2, H])
        rowsum = sb("rowsum", [P, 2, H])
        dimg = sb("dimg", [P, 2, H])
        pimg = sb("pimg", [P, 2, H])
        total = sb("total", [P, 2, H])
        rinv = sb("rinv", [P, 2, H])
        pimgT = sb("pimgT", [H, P])
        attnT_hi = sb("attnT_hi", [P, C, 2 * P], F32R)
        attnT_lo = sb("attnT_lo", [P, C, 2 * P], F32R)
        x1T = sb("x1T", [P, C, 2 * P])
        x1nat = sb("x1nat", [P, 2, D])
        xw = sb("xw", [P, PAIRS, PAIRS, C, 2, STEPS])
        pre = sb("pre", [P, C, Q])
        hist = sb("hist", [P, 2, C, B, HALF])
        x1out = sb("x1out", [P, D])
        osb = sb("osb", [P, D])
        imgT = sb("imgT", [P, C, B])

        dense = [ctx.enter_context(nc.psum_tensor(f"dense{i}", [P, BANK], F32)) for i in range(2)]
        scores = [ctx.enter_context(nc.psum_tensor(f"scores{i}", [P, BANK], F32)) for i in range(2)]
        turned = [ctx.enter_context(nc.psum_tensor(f"turned{i}", [P, BANK], F32)) for i in range(2)]
        pv = ctx.enter_context(nc.psum_tensor("pv", [P, BANK], F32))
        rec = ctx.enter_context(nc.psum_tensor("rec", [P, BANK], F32))

        kT_hi, kT_lo = attnT_hi, attnT_lo
        rinvx = x1nat[:, 0, :].rearrange("p (h q) -> p h q", h=H)
        rbc = x1nat[:, 1, :].rearrange("p (c q) -> p c q", c=C)
        headmask = qT[:, 0:2, :].rearrange("p a n -> p (a n)")
        vimg_all = qT[:, 2:4, :].rearrange("p a n -> p (a n)")
        vimg_heads = x1nat[:, 0, :]
        cond_sb = osb[0:B, :]
        image_w = [wx, wh]
        xw_flat = xw[:].rearrange("p a b c e t -> p (a b c e t)")
        W2 = 3 * D // 2
        raw_qkv = [xw_flat[:, W2 * i:W2 * (i + 1)] for i in range(5)]
        raw_qkv += [probs_held[:, 0:W2], x1T[:].rearrange("p f t -> p (f t)")[:, 0:W2],
                    msk[:].rearrange("p e n -> p (e n)")[:, 0:W2]]
        raw_proj = [vst[:, c // 2, 2 + c % 2, :] for c in range(C)]
        imgTx = rbc.rearrange("p f (b h) -> p f b h", b=B)
        pre_all = pre[:].rearrange("p f q -> p (f q)")
        x1kept = xw[:].rearrange("p a b f e t -> p a b (f e t)").rearrange(
            "p a b (k f e t) -> p a b k f e t", k=2, f=C, e=2)
        x1step = qT[:].rearrange("p f t -> p (f t)").rearrange("p (k f b t) -> p k f b t", k=2, f=C, b=B)

        kq_dram = nc.dram_tensor("kq_dram", [3, PAIRS, P, C, 2, P + S], F32, kind="Internal").ap()
        v_dram = nc.dram_tensor("v_dram", [B, S, D], F32, kind="Internal").ap()
        vimg_dram = nc.dram_tensor("vimg_dram", [B, H, D], F32, kind="Internal").ap()
        x1_dram = nc.dram_tensor("x1_dram", [B, S, D], F32, kind="Internal").ap()

        weights_loaded = sem("weights_loaded")
        qkv_loaded = [sem(f"qkv_loaded{i}") for i in range(2 * C)]
        proj_loaded = sem("proj_loaded")
        bv_loaded = sem("bv_loaded")
        high_ready = sem("high_ready")
        low_ready = sem("low_ready")
        setup_loaded = sem("setup_loaded")
        setup_turned = sem("setup_turned")
        setup_copied = sem("setup_copied")
        setup_product = sem("setup_product")
        zeroed = sem("zeroed")
        image_ready = sem("image_ready")
        kimg_ready = sem("kimg_ready")
        x_loaded = [sem(f"x_loaded{i}") for i in range(2)]
        staged = [sem(f"staged{e}") for e in range(2)]
        mask_scaled = sem("mask_scaled")
        mask_ready = sem("mask_ready")
        q_high = sem("q_high")
        k_high = sem("k_high")
        q_whole = sem("q_whole")
        tile_loaded = [sem(f"tile_loaded{i}") for i in range(max(TILES))]
        dense_ready = sem("dense_ready")
        dense_copied = [sem(f"dense_copied{i}") for i in range(2)]
        scores_ready = sem("scores_ready")
        shifted_ready = sem("shifted_ready")
        probs_ready = sem("probs_ready")
        turned_ready = sem("turned_ready")
        turned_copied = [sem(f"turned_copied{i}") for i in range(2)]
        pv_done = sem("pv_done")
        dimg_ready = sem("dimg_ready")
        pimg_ready = sem("pimg_ready")
        total_ready = sem("total_ready")
        recip_ready = sem("recip_ready")
        rinv_ready = sem("rinv_ready")
        attn_summed = sem("attn_summed")
        attn_ready = sem("attn_ready")
        attn_high = sem("attn_high")
        attn_split = sem("attn_split")
        xT_high = sem("xT_high")
        xT_low = sem("xT_low")
        x_used = sem("x_used")
        x1_kept = sem("x1_kept")
        x1_set_out = [sem(f"x1_set_out{i}") for i in range(2)]
        kq_stored = [sem(f"kq_stored{i}") for i in range(2)]
        v_stored = sem("v_stored")
        x1_stored = sem("x1_stored")
        x1out_loaded = sem("x1out_loaded")
        rec_ready = sem("rec_ready")
        rec_turned = sem("rec_turned")
        pre_ready = sem("pre_ready")
        h_ready = sem("h_ready")
        out_stored = sem("out_stored")

        def held(p):
            n = P * (p + 1)
            return probs_held[:, 0:HELD[p] * n].rearrange("p (a n) -> p a n", n=n)

        def heads_tile(p, k):
            n = HC * P * (p + 2)
            slot = k % TILES[p]
            return kq_tiles[:, n * slot:n * slot + n].rearrange("p (j n) -> p j n", j=HC)

        def tile_loads(p, r, k):
            before = [sum(PAIRS * (t % TILES[b] == k % TILES[p]) for b in range(p) for t in range(2 * C))]
            a_trip = sum(t % TILES[p] == k % TILES[p] for t in range(2 * C))
            return r * (a_trip * 3 * 16) + (before[0] + k // TILES[p] + 1) * 3 * 16

        def folded(ap):
            return ap.rearrange("p (j f c) -> p f j c", j=C, f=C)

        def trip(p, r):
            return r + PAIRS * p

        def job(p, r, name, i):
            return r * JOB[p]["count"] + (base[p] + JOB[p][name, i])

        def wait_dense(eng, p, r, name, i):
            eng.wait_ge(dense_ready, job(p, r, name, i) + 1)

        def wait_copied(eng, p, r, name, i):
            n = JOB[p][name, i]
            eng.wait_ge(dense_copied[n % 2], since(r * (JOB[p]["count"] // 2) + (base[p] // 2 + n // 2 + 1)))

        def wait_bank(eng, p, r, name, i):
            n = JOB[p][name, i]
            eng.wait_ge(dense_copied[n % 2], since(r * (JOB[p]["count"] // 2) + (base[p] // 2 + n // 2)))

        def bank(p, name, i):
            return dense[JOB[p][name, i] % 2]

        def copied(p, name, i):
            return dense_copied[JOB[p][name, i] % 2]

        def staged_by(p, r):
            return r * 32 + 32 if p == 0 else r * 48 + (PAIRS * 32 + (p - 1) * PAIRS * 48 + 48)

        def step_count(p, r, s):
            return r * STEPS + ((p - 1) * PAIRS * STEPS + s)

        def rec_bank(p, i):
            return scores[0] if p == BLOCKS and i % 2 == 0 else rec

        def split_product(out, hi, lo, moving_hi, moving_lo, first, last):
            pe = nc.tensor
            pe.matmul(out, hi, moving_hi, start=first, stop=False)
            pe.matmul(out, hi, moving_lo, start=False, stop=False)
            return pe.matmul(out, lo, moving_hi, start=False, stop=last)

        def chunk_halves(e):
            return [(slice(None), slice(C // 2 * k, C // 2 * (k + 1)), slice(P * e, P * e + P)) for k in range(2)]

        def since(n):
            return n + LEAD

        def after_vimg(n):
            return n + 16

        def alone(eng):
            eng.nop(nofuse=True)

        block = ctx.enter_context(nc.Block())

        @block.sync
        def _(sp):
            for tile, a in ((ident[:], ident_in), (cond_sb, cond), (ukb[:], uk_b), (headmask, headmask_in),
                            (bv[:], uv_b.rearrange("(a n) -> a n", a=1).broadcast_to([P, D])),
                            (bqk[:], b_qk), (bproj[:], b_proj), (bx[:], b_h), (causal[:], causal_in),
                            (vst[:, 0, :, :], uk_w), (vst[:, 1, :, :], uv_w)):
                sp.dma_start(tile, a).then_inc(setup_loaded, 16)
            for i in range(2 * C):
                f, half = divmod(i, 2)
                sp.dma_start(raw_qkv[i], w_qkv[:, f, W2 * half:W2 * (half + 1)]).then_inc(qkv_loaded[i], 16)
            sp.wait_ge(setup_turned, 2 * C)
            for c in range(C):
                sp.dma_start(raw_proj[c], w_proj[:, c, :]).then_inc(proj_loaded, 16)

            for p in range(BLOCKS):
                with sp.Fori(0, PAIRS) as r:
                    g = trip(p, r)
                    for k in range(2):
                        sp.wait_ge(x_used, since(g * 2 + (k - 1)))
                        alone(sp)
                        sp.dma_start(xin[:, 2 * k:2 * k + 2, :], x[bass.ds(g, 1), :, 2 * k:2 * k + 2, :]
                                     .rearrange("a q c t -> q (a c) t")).then_inc(x_loaded[k], 16)
                    sp.wait_ge(attn_summed, since(g * 2))
                    alone(sp)
                    if p == 0:
                        sp.wait_ge(low_ready, 2 * C)
                        for stored in (v_stored, x1_stored, out_stored):
                            sp.wait_ge(stored, after_vimg(0))
                    sp.wait_ge(v_stored, after_vimg(g * 32) if p < BLOCKS - 1 else after_vimg(V_STORES))
                    for e in range(2):
                        batch = bass.ds(r * 2 + e, 1)
                        sp.dma_start(msk[:, e, 0:P * (p + 1)], mask[batch, 0, 0, 0:P * (p + 1)]
                                     .broadcast_to([P, P * (p + 1)])).then_inc(staged[e], 16)
                        sp.dma_start(vimg[:, e, :], vimg_dram[batch, :, :]).then_inc(staged[e], 16)
                        if p:
                            sp.dma_start(vst[:, e, 0:p, :], v_dram[batch, 0:P * p, :]
                                         .rearrange("a (n q) d -> a q n d", q=P)).then_inc(staged[e], 16)
                    for k in range(2 * C):
                        e, c = divmod(k, C)
                        if k < 2:
                            for name, parts, at in (("q", (qT_hi, qT_hi, qT_lo), 0),
                                                    ("k", (kT_hi, kT_lo, kT_hi), P * (p + 1))):
                                wait_copied(sp, p, r, name, 2 * k)
                                wait_copied(sp, p, r, name, 2 * k + 1)
                                alone(sp)
                                for part, src in enumerate(parts):
                                    sp.dma_start(kq_dram[part, bass.ds(r, 1), :, 2 * k:2 * k + 2, :, at:at + P]
                                                 .rearrange("a q c e t -> q (a c e) t"),
                                                 src[:, 2 * k:2 * k + 2, :].bitcast(F32)
                                                 .rearrange("p c (e t) -> p (c e) t", e=2)).then_inc(kq_stored[k], 16)
                        if k in (0, 2):
                            sp.wait_ge(kq_stored[k // 2], g * KQ_STORES + KQ_STORES)
                            alone(sp)
                        sp.wait_ge(scores_ready, since(g * UNITS + HC * max(0, k - TILES[p] + 1)))
                        alone(sp)
                        for part in range(3):
                            sp.dma_start(heads_tile(p, k)[Q * part:Q * part + Q].bitcast(F32),
                                         kq_dram[part, bass.ds(r, 1), :, c, e, 0:P + P * (p + 1)]
                                         .rearrange("a (j d) t -> d (a j) t", d=Q)).then_inc(tile_loaded[k % TILES[p]], 16)

        @block.gpsimd
        def _(pool):
            for lead in [*dense_copied, *turned_copied, shifted_ready, turned_ready, pv_done, attn_summed,
                         attn_ready, scores_ready, x_used]:
                pool.sem_inc(lead, LEAD)
            pool.wait_ge(image_ready, 2)
            for rows, stored in ((slice(0, 3 * Q // 2), v_stored), (slice(3 * Q // 2, 3 * Q), x1_stored),
                                 (slice(3 * Q, P), out_stored)):
                pool.dma_start(vimg_dram.rearrange("b h d -> (b h) d")[rows, :], vimg_heads[rows, :]).then_inc(stored, 16)
            pool.dma_start(bv[:], b_v.rearrange("(a n) -> a n", a=1).broadcast_to([P, D])).then_inc(bv_loaded, 16)
            for tile, w in ((wx, w_x), (wh, w_h)):
                pool.dma_start(tile[:], w).then_inc(weights_loaded, 16)
            pool.wait_ge(setup_loaded, SETUP_LOADS)

            def load_x1(p, r, k):
                pool.dma_start(x1out[:], x1_dram[:, bass.ds(r * STEPS + ((p - 1) * P + k * HALF), HALF), :]
                               ).then_inc(x1out_loaded, 16)

            for p in range(BLOCKS + 1):
                if p:
                    pool.wait_ge(x1_stored, after_vimg(p * PAIRS * 32))
                with pool.Fori(0, PAIRS) as r:
                    g = trip(p, r)
                    for kind, i in order(p):
                        if kind == "xsplit" and i == 0:
                            for e in range(2):
                                pool.wait_ge(staged[e], staged_by(p, r))
                                alone(pool)
                                pool.tensor_scalar(msk[:, e, 0:P * (p + 1)], msk[:, e, 0:P * (p + 1)], ROOT, None,
                                                   ALU.mult).then_inc(mask_scaled, 1)
                                pool.wait_ge(mask_scaled, g * 2 + (e + 1))
                                pool.tensor_tensor(msk[:, e, P * p:P * (p + 1)], msk[:, e, P * p:P * (p + 1)],
                                                   causal[:], ALU.add).then_inc(mask_ready, 1)
                        elif kind == "proj" and i % 2:
                            wait_copied(pool, p, r, "proj", i - 1)
                            wait_copied(pool, p, r, "proj", i)
                            alone(pool)
                            pool.sem_inc(x_used, 1)
                        elif kind == "keep":
                            if i == 0:
                                pool.wait_ge(pre_ready, step_count(p, r, STEPS))
                            alone(pool)
                            pool.tensor_copy(x1kept[:, :, bass.ds(r, 1), :, i, :, :].rearrange("p a b k e t -> p (a b) k e t"),
                                             x1T[:, i, :].rearrange("p (e a k t) -> p a k e t", e=2, a=PAIRS, k=2)
                                             ).then_inc(x1_kept, 1)
                        elif kind == "k" and i == C // 2:
                            wait_copied(pool, p, r, "q", C - 2)
                            wait_copied(pool, p, r, "q", C - 1)
                            alone(pool)
                            pool.tensor_tensor(qT[:], qT_hi[:].bitcast(F32), qT_lo[:].bitcast(F32), ALU.add).then_inc(q_whole, 1)
                        elif kind == "head" and i == 2 and p < BLOCKS - 1:
                            for e in range(2):
                                wait_copied(pool, p, r, "v", 2 + e)
                            alone(pool)
                            for e in range(2):
                                pool.dma_start(v_dram[bass.ds(r * 2 + e, 1), P * p:P * p + P, :],
                                               vst[:, e, p, :]).then_inc(v_stored, 16)
                        elif kind == "x1n":
                            wait_copied(pool, p, r, "x1n", i)
                            alone(pool)
                            pool.dma_start(x1_dram[bass.ds(r * 2 + i, 1), P * p:P * p + P, :],
                                           x1nat[:, i, :]).then_inc(x1_stored, 16)
                        elif kind == "step" and i == 0:
                            load_x1(p, r, 0)
                        elif kind == "out":
                            wait_copied(pool, p, r, "out", i)
                            alone(pool)
                            pool.dma_start(out[:, bass.ds(r * STEPS + ((p - 1) * P + i * HALF), HALF), :], osb[:]
                                           ).then_inc(out_stored, 16)
                            if i == 0:
                                load_x1(p, r, 1)
            pool.wait_ge(out_stored, after_vimg(16 * 2 * PAIRS * BLOCKS))
            pool.wait_ge(v_stored, after_vimg(V_STORES))
            pool.wait_ge(x1_stored, after_vimg(32 * PAIRS * BLOCKS))

        @block.scalar
        def _(act):
            for i in range(2 * C):
                f, half = divmod(i, 2)
                act.wait_ge(qkv_loaded[i], 16)
                act.copy(wqkv_hi[:, f, W2 * half:W2 * (half + 1)], raw_qkv[i]).then_inc(high_ready, 1)
            act.wait_ge(setup_loaded, SETUP_LOADS)
            act.wait_ge(proj_loaded, 16 * C)
            for c in range(C):
                act.copy(wproj_hi[:, c, :], raw_proj[c]).then_inc(high_ready, 1)
            for p in range(BLOCKS + 1):
                n = P * (p + 1)

                def head(r, u):
                    g = trip(p, r)
                    v = u - KEYLAG[p]
                    if 0 <= v < UNITS and v % 2:
                        act.wait_ge(turned_ready, since(g * UNITS + (v + 1)))
                        act.wait_ge(pv_done, since(g * UNITS + (v - 1)))
                        act.copy(probsT[:, 1, 0:n], turned[1][:, 0:n]).then_inc(turned_copied[1], 1)
                    if u < UNITS:
                        e, h = divmod(u, H)
                        act.wait_ge(shifted_ready, since(g * UNITS + (u + 1)))
                        act.activation(held(p)[:, u % HELD[p], :], held(p)[:, u % HELD[p], :], ACT.Exp, scale=-1.0,
                                       bias=nmax[:, e, h:h + 1], accum_out=rowsum[:, e, h:h + 1]).then_inc(probs_ready, 1)

                with act.Fori(0, PAIRS) as r:
                    g = trip(p, r)
                    for kind, i in order(p):
                        if kind == "xsplit":
                            act.wait_ge(x_loaded[i], g * 16 + 16)
                            act.copy(xT_hi[:, 2 * i:2 * i + 2, :], xin[:, 2 * i:2 * i + 2, :]).then_inc(xT_high, 1)
                        elif kind == "q":
                            wait_dense(act, p, r, "q", i)
                            act.activation(qT_hi[:, i, :], bank(p, kind, i)[:, 0:2 * P], ACT.Identity,
                                           bias=bqk[:, 0, i:i + 1]).then_inc(q_high, 1)
                        elif kind == "k":
                            wait_dense(act, p, r, "k", i)
                            act.activation(kT_hi[:, i, :], bank(p, kind, i)[:, 0:2 * P], ACT.Identity,
                                           bias=bqk[:, 1, i:i + 1]).then_inc(k_high, 1)
                        elif kind == "head":
                            head(r, i)
                        elif kind == "imgprob":
                            act.wait_ge(dimg_ready, g * 2 + (i + 1))
                            act.activation(pimg[:, i, :], dimg[:, i, :], ACT.Exp).then_inc(pimg_ready, 1)
                        elif kind == "imgturn":
                            wait_dense(act, p, r, "pimgt", i)
                            act.copy(pimgT[:], bank(p, "pimgt", i)[0:H, 0:P]).then_inc(copied(p, "pimgt", i), 1)
                        elif kind == "rowturn":
                            wait_dense(act, p, r, "rbc", i)
                            act.copy(x1nat[:, 1, :], bank(p, "rbc", i)[:, :]
                                     ).then_inc(copied(p, "rbc", i), 1)
                        elif kind == "norm":
                            for stored in kq_stored:
                                act.wait_ge(stored, g * KQ_STORES + KQ_STORES)
                            for k, mine in enumerate(chunk_halves(i)):
                                act.wait_ge(attn_ready, since(g * 4 + (i * 2 + k + 1)))
                                act.copy(attnT_hi[mine], x1T[mine]).then_inc(attn_high, 1)
                        elif kind == "wx":
                            wait_dense(act, p, r, "wx", i)
                            cells = xw[:, bass.ds(r, 1), :, i] if p % 2 == 0 else xw[:, :, bass.ds(r, 1), i]
                            act.activation(cells.rearrange("p a g e t -> p (a g) e t"),
                                           bank(p, kind, i)[:, 0:2 * P].rearrange("p (e g t) -> p g e t", e=2, g=PAIRS),
                                           ACT.Identity, bias=bx[:, i:i + 1]).then_inc(copied(p, kind, i), 1)
                        elif kind == "x1n":
                            wait_dense(act, p, r, "x1n", i)
                            act.copy(folded(x1nat[:, i, :]),
                                     bank(p, kind, i)[:, :].rearrange("p (f j c) -> p f j c", f=C, j=C)
                                     ).then_inc(copied(p, kind, i), 1)
                        elif kind == "step":
                            act.wait_ge(pre_ready, step_count(p, r, i) + 1)
                            act.activation(hist[:, i // HALF, :, :, i % HALF], pre[:, :, 0:B], ACT.Tanh).then_inc(h_ready, 1)

        @block.vector
        def _(dve):
            def split_qkv(i):
                f, half = divmod(i, 2)
                part = slice(W2 * half, W2 * (half + 1))
                dve.wait_ge(high_ready, i + 1)
                dve.tensor_tensor(wqkv_lo[:, f, part], raw_qkv[i], wqkv_hi[:, f, part].bitcast(F32), ALU.subtract
                                  ).then_inc(low_ready, 1)

            dve.memset(rec[:], 0.0).then_inc(zeroed, 1)
            dve.memset(kimg[:], 0.0).then_inc(zeroed, 1)
            dve.wait_ge(zeroed, 2)
            for e, banks in ((0, scores + turned), (1, dense + [pv, scores[1]])):
                for f in range(C):
                    dve.wait_ge(setup_turned, e * C + f + 1)
                    dve.tensor_copy(image_w[e][:, f, :], banks[f][:, :]).then_inc(setup_copied, 1)
            dve.wait_ge(setup_turned, 2 * C + 1)
            dve.tensor_copy(imgT[:], scores[0][:, 0:C * B].rearrange("p (f b) -> p f b", f=C)).then_inc(setup_copied, 1)
            dve.tensor_copy(hist[:, 1, :, :, HALF - 1],
                            scores[0][:, 0:C * B].rearrange("p (f b) -> p f b", f=C)).then_inc(h_ready, 1)
            dve.wait_ge(setup_copied, 2 * C + 1)
            dve.tensor_copy(imgTx, imgT[:].unsqueeze(3).broadcast_to([P, C, B, H])).then_inc(setup_copied, 1)
            for i in range(C):
                split_qkv(i)
            dve.wait_ge(setup_product, 1)
            for j in range(HC):
                rows = slice(Q * j, Q * j + Q)
                dve.tensor_tensor(kimg[rows, :, :, j], scores[1][rows, 0:C * B].rearrange("p (c b) -> p c b", c=C),
                                  ukb[rows, :].unsqueeze(2).broadcast_to([Q, C, B]), ALU.add).then_inc(kimg_ready, 1)
            for i in range(C, 2 * C):
                split_qkv(i)
            dve.wait_ge(setup_product, 2)
            dve.tensor_tensor(vimg_all, turned[0][:, :], bv[:], ALU.add).then_inc(image_ready, 1)
            dve.wait_ge(image_ready, 1)
            dve.tensor_tensor(vimg_heads, vimg_all, headmask, ALU.mult).then_inc(image_ready, 1)
            for c in range(C):
                dve.wait_ge(high_ready, 2 * C + c + 1)
                dve.tensor_tensor(wproj_lo[:, c, :], raw_proj[c], wproj_hi[:, c, :].bitcast(F32), ALU.subtract
                                  ).then_inc(low_ready, 1)

            for p in range(BLOCKS + 1):
                n = P * (p + 1)
                if p == BLOCKS:
                    dve.wait_ge(x1_kept, C * PAIRS)
                elif p:
                    for i in range(2):
                        dve.wait_ge(dense_copied[i], since(base[p] // 2))

                def head(r, u):
                    g = trip(p, r)
                    if u < UNITS:
                        e, h = divmod(u, H)
                        dve.wait_ge(scores_ready, since(g * UNITS + (u + 1)))
                        dve.wait_ge(turned_ready, since(g * UNITS + (u - HELD[p] + 1)))
                        if h == 0:
                            dve.wait_ge(mask_ready, g * 2 + (e + 1))
                        alone(dve)
                        dve.tensor_tensor_reduce(out=held(p)[:, u % HELD[p], :], in0=scores[u % 2][:, 0:n],
                                                 in1=msk[:, e, 0:n], scale=-SCALE, scalar=nimg[:, e, h:h + 1],
                                                 op0=ALU.add, op1=ALU.min, accum_out=nmax[:, e, h:h + 1]
                                                 ).then_inc(shifted_ready, 1)
                    v = u - KEYLAG[p]
                    if 0 <= v < UNITS and v % 2 == 0:
                        dve.wait_ge(turned_ready, since(g * UNITS + (v + 1)))
                        dve.wait_ge(pv_done, since(g * UNITS + (v - 1)))
                        dve.tensor_copy(probsT[:, 0, 0:n], turned[0][:, 0:n]).then_inc(turned_copied[0], 1)

                def set_out(r, half):
                    alone(dve)
                    dve.tensor_copy(x1step[:, half].rearrange("p f b t -> p f (b t)")
                                    .rearrange("p f (g u) -> p g f u", g=PAIRS),
                                    x1kept[:, bass.ds(r, 1), :, half].rearrange("p a g f e t -> p (a g) f (e t)")
                                    ).then_inc(x1_set_out[half], 1)

                with dve.Fori(0, PAIRS) as r:
                    g = trip(p, r)
                    for kind, i in order(p):
                        if kind == "xsplit":
                            dve.wait_ge(xT_high, g * 2 + (i + 1))
                            half = slice(2 * i, 2 * i + 2)
                            dve.tensor_tensor(xT_lo[:, half, :], xin[:, half, :], xT_hi[:, half, :].bitcast(F32), ALU.subtract
                                              ).then_inc(xT_low, 1)
                        if kind in ("q", "k"):
                            high, hi, lo = (q_high, qT_hi, qT_lo) if kind == "q" else (k_high, kT_hi, kT_lo)
                            t = int(kind == "k")
                            dve.wait_ge(high, g * C + (i + 1))
                            dve.scalar_tensor_tensor(out=lo[:, i, :], in0=bank(p, kind, i)[:, 0:2 * P],
                                                     scalar=bqk[:, t, i:i + 1], in1=hi[:, i, :].bitcast(F32),
                                                     op0=ALU.add, op1=ALU.subtract).then_inc(copied(p, kind, i), 1)
                        elif kind == "v":
                            wait_dense(dve, p, r, "v", i)
                            if i == 0:
                                dve.wait_ge(v_stored, after_vimg(g * 32) if p < BLOCKS - 1 else after_vimg(V_STORES))
                                dve.wait_ge(bv_loaded, 16)
                            e, half = divmod(i, 2)
                            cols = slice(half * D // 2, (half + 1) * D // 2)
                            dve.tensor_tensor(vst[:, e, p, cols], bank(p, kind, i)[:, 0:D // 2], bv[:, cols], ALU.add
                                              ).then_inc(copied(p, kind, i), 1)
                        elif kind == "imgscore":
                            wait_dense(dve, p, r, "imgscore", i)
                            dve.tensor_scalar(nimg[:, i, :], bank(p, kind, i)[:, 0:H], -SCALE, None, ALU.mult
                                              ).then_inc(copied(p, kind, i), 1)
                            wait_copied(dve, p, r, "imgscore", i)
                        elif kind == "head":
                            head(r, i)
                        elif kind == "imgprob":
                            dve.wait_ge(shifted_ready, since(g * UNITS + (i + 1) * H))
                            dve.tensor_tensor(dimg[:, i, :], nmax[:, i, :], nimg[:, i, :], ALU.subtract
                                              ).then_inc(dimg_ready, 1)
                        elif kind == "imgturn":
                            dve.wait_ge(pimg_ready, g * 2 + (i + 1))
                            dve.wait_ge(probs_ready, g * UNITS + (i + 1) * H)
                            dve.tensor_tensor(total[:, i, :], rowsum[:, i, :], pimg[:, i, :], ALU.add
                                              ).then_inc(total_ready, 1)
                            dve.wait_ge(total_ready, g * 2 + (i + 1))
                            dve.reciprocal(rinv[:, i, :], total[:, i, :]).then_inc(recip_ready, 1)
                            dve.wait_ge(recip_ready, g * 2 + (i + 1))
                            dve.wait_ge(x1_stored, after_vimg(g * 32))
                            dve.tensor_copy(rinvx, rinv[:, i, :].unsqueeze(2).broadcast_to([P, H, Q])
                                            ).then_inc(rinv_ready, 1)
                        elif kind == "norm":
                            dve.wait_ge(attn_summed, since(g * 2 + (i + 1)))
                            wait_copied(dve, p, r, "rbc", i)
                            for k, mine in enumerate(chunk_halves(i)):
                                chunks = mine[1]
                                dve.tensor_tensor(x1T[mine], pv[:, :].rearrange("p (c q) -> p c q", c=C)[:, chunks, :],
                                                  rbc[:, chunks, :], ALU.mult).then_inc(attn_ready, 1)
                            for k, mine in enumerate(chunk_halves(i)):
                                dve.wait_ge(attn_high, g * 4 + (i * 2 + k + 1))
                                dve.tensor_tensor(attnT_lo[mine], x1T[mine], attnT_hi[mine].bitcast(F32),
                                                  ALU.subtract).then_inc(attn_split, 1)
                        elif kind == "proj":
                            wait_dense(dve, p, r, "proj", i)
                            dve.scalar_tensor_tensor(out=x1T[:, i, :], in0=bank(p, kind, i)[:, 0:2 * P],
                                                     scalar=bproj[:, i:i + 1], in1=xin[:, i, :], op0=ALU.add, op1=ALU.add
                                                     ).then_inc(copied(p, kind, i), 1)
                        elif kind == "step":
                            t = step_count(p, r, i)
                            if p == BLOCKS and i == 0:
                                set_out(r, 0)
                            dve.wait_ge(rec_ready, t + 1)
                            dve.transpose(pre_all, rec_bank(p, i)[:, 0:P]).then_inc(rec_turned, 1)
                            dve.wait_ge(rec_turned, t + 1)
                            if p == BLOCKS:
                                dve.tensor_tensor(pre[:, :, 0:B], pre[:, :, 0:B],
                                                  bx[:].unsqueeze(2).broadcast_to([P, C, B]), ALU.add).then_inc(pre_ready, 1)
                                if i == 0:
                                    set_out(r, 1)
                            else:
                                cells = xw[:, :, bass.ds(r, 1), :, :, i] if p % 2 else xw[:, bass.ds(r, 1), :, :, :, i]
                                sums = pre[:, :, 0:B].rearrange("p f (b e) -> p f b e", e=2)
                                dve.tensor_tensor(sums, sums, cells.rearrange("p a g f e -> p f (a g) e"),
                                                  ALU.add).then_inc(pre_ready, 1)
                        elif kind == "out":
                            o = r * 2 + ((p - 1) * PAIRS * 2 + i)
                            wait_dense(dve, p, r, "out", i)
                            dve.wait_ge(x1out_loaded, o * 16 + 16)
                            dve.wait_ge(out_stored, after_vimg(o * 16))
                            dve.tensor_tensor(folded(osb[:]),
                                              bank(p, kind, i)[:, :].rearrange("p (f j c) -> p f j c", f=C, j=C),
                                              folded(x1out[:]), ALU.add).then_inc(copied(p, kind, i), 1)

        @block.tensor
        def _(pe):
            pe.wait_ge(setup_loaded, SETUP_LOADS)
            for e, banks in ((0, scores + turned), (1, dense + [pv, scores[1]])):
                for f in range(C):
                    if (e, f) == (1, C - 1):
                        pe.wait_ge(setup_copied, 2)
                    for o in range(C):
                        last = pe.transpose(banks[f][:, P * o:P * o + P], vst[:, e, o, P * f:P * f + P], ident[:])
                    last.then_inc(setup_turned, 1)
            pe.wait_ge(setup_copied, 2 * C)
            for f in range(C):
                last = pe.transpose(scores[0][:, B * f:B * f + B], cond_sb[:, P * f:P * f + P], ident[0:B, 0:B])
            last.then_inc(setup_turned, 1)
            pe.wait_ge(setup_copied, 2 * C + 1)
            for c in range(C):
                for f in range(C):
                    last = pe.matmul(scores[1][:, B * c:B * c + B], image_w[0][:, f, P * c:P * c + P], imgT[:, f, :],
                                     start=f == 0, stop=f == C - 1)
            last.then_inc(setup_product, 1)
            pe.wait_ge(setup_copied, 2 * C + 2)
            for f in range(C):
                last = pe.matmul(turned[0][:, :], rbc[:, f, :], image_w[1][:, f, :],
                                 start=f == 0, stop=f == C - 1)
            last.then_inc(setup_product, 1)
            pe.wait_ge(image_ready, 2)
            pe.wait_ge(kimg_ready, HC)
            pe.wait_ge(h_ready, 1)
            pe.wait_ge(zeroed, 2)

            for p in range(BLOCKS + 1):
                n = P * (p + 1)

                def head(r, u):
                    g = trip(p, r)
                    if u < UNITS:
                        e, h = divmod(u, H)
                        c, j = divmod(h, HC)
                        if h == 0:
                            pe.wait_ge(staged[e], staged_by(p, r))
                        k = C * e + c
                        if j == 0:
                            pe.wait_ge(tile_loaded[k % TILES[p]], tile_loads(p, r, k))
                        pe.wait_ge(shifted_ready, since(g * UNITS + (u - 1)))
                        pe.matmul(scores[u % 2][:, 0:n], heads_tile(p, k)[0:3 * Q, j, 0:P],
                                  heads_tile(p, k)[0:3 * Q, j, P:P + n], start=True, stop=True
                                  ).then_inc(scores_ready, 1)
                    if KEYLAG[p] <= u < UNITS + KEYLAG[p]:
                        v = u - KEYLAG[p]
                        pe.wait_ge(probs_ready, g * UNITS + (v + 1))
                        pe.wait_ge(turned_copied[v % 2], since(g * H + (v // 2)))
                        for k in range(p + 1):
                            last = pe.transpose(turned[v % 2][:, P * k:P * k + P], held(p)[:, v % HELD[p], P * k:P * k + P], ident[:])
                        last.then_inc(turned_ready, 1)
                    if u >= PVLAG[p]:
                        v = u - PVLAG[p]
                        e, h = divmod(v, H)
                        c, j = divmod(h, HC)
                        pe.wait_ge(turned_copied[v % 2], since(g * H + (v // 2 + 1)))
                        if h == 0:
                            pe.wait_ge(attn_ready, since(g * 4 + e * 2))
                        for k in range(p + 1):
                            last = pe.matmul(pv[Q * j:Q * j + Q, P * c:P * c + P], vst[:, e, k, DH * h:DH * h + DH],
                                             probsT[:, v % 2, P * k:P * k + P], start=c == 0 and k == 0, stop=False,
                                             skip_group_check=True)
                        last.then_inc(pv_done, 1)

                with pe.Fori(0, PAIRS) as r:
                    g = trip(p, r)
                    for kind, i in order(p):
                        if kind in JOBS and kind != "out":
                            wait_bank(pe, p, r, kind, i)
                            d = bank(p, kind, i)
                        if kind in ("q", "k"):
                            if kind == "q" and i == 0:
                                pe.wait_ge(low_ready, 2 * C)
                            w0 = D * (kind == "k") + P * i
                            for f in range(C):
                                if kind == "q" and i == 0 and f % 2 == 0:
                                    pe.wait_ge(xT_low, g * 2 + (f // 2 + 1))
                                last = split_product(d[:, 0:2 * P], wqkv_hi[:, f, w0:w0 + P], wqkv_lo[:, f, w0:w0 + P],
                                                     xT_hi[:, f, :], xT_lo[:, f, :], f == 0, f == C - 1)
                            last.then_inc(dense_ready, 1)
                        elif kind == "v":
                            e, half = divmod(i, 2)
                            w0 = 2 * D + half * D // 2
                            for f in range(C):
                                last = split_product(d[:, 0:D // 2], xT_hi[:, f, P * e:P * e + P], xT_lo[:, f, P * e:P * e + P],
                                                     wqkv_hi[:, f, w0:w0 + D // 2], wqkv_lo[:, f, w0:w0 + D // 2],
                                                     f == 0, f == C - 1)
                            last.then_inc(dense_ready, 1)
                        elif kind == "imgscore":
                            pe.wait_ge(q_whole, g + 1)
                            for c in range(C):
                                last = pe.matmul(d[:, HC * c:HC * c + HC], qT[:, c, P * i:P * i + P],
                                                 kimg[:, c, bass.ds(r * 2 + i, 1), :], start=True, stop=True)
                            last.then_inc(dense_ready, 1)
                        elif kind == "head":
                            head(r, i)
                        elif kind == "imgturn":
                            pe.wait_ge(pimg_ready, g * 2 + (i + 1))
                            wait_bank(pe, p, r, "pimgt", i)
                            pe.transpose(bank(p, "pimgt", i)[0:H, 0:P], pimg[:, i, :], ident[:]).then_inc(dense_ready, 1)
                        elif kind == "rowturn":
                            pe.wait_ge(rinv_ready, g * 2 + (i + 1))
                            wait_bank(pe, p, r, "rbc", i)
                            for c in range(C):
                                last = pe.transpose(bank(p, "rbc", i)[:, P * c:P * c + P],
                                                    rinvx[:, HC * c:HC * c + HC, :].rearrange("p j q -> p (j q)"),
                                                    ident[:])
                            last.then_inc(dense_ready, 1)
                        elif kind == "norm":
                            wait_copied(pe, p, r, "pimgt", i)
                            for c in range(C):
                                last = pe.matmul(pv[:, P * c:P * c + P], vimg[:, i, P * c:P * c + P], pimgT[:],
                                                 start=False, stop=True, skip_group_check=True)
                            last.then_inc(attn_summed, 1)
                        elif kind == "proj":
                            if i == 0:
                                pe.wait_ge(low_ready, 3 * C)
                            for c in range(C):
                                if i == 0 and c % 2 == 0:
                                    pe.wait_ge(attn_split, g * 4 + (3 + c // 2))
                                last = split_product(d[:, 0:2 * P], wproj_hi[:, c, P * i:P * i + P],
                                                     wproj_lo[:, c, P * i:P * i + P], attnT_hi[:, c, :],
                                                     attnT_lo[:, c, :], c == 0, c == C - 1)
                            last.then_inc(dense_ready, 1)
                        elif kind == "wx":
                            if i == 0:
                                pe.wait_ge(weights_loaded, WEIGHT_LOADS)
                                wait_copied(pe, p, r, "proj", C - 2)
                                wait_copied(pe, p, r, "proj", C - 1)
                            for f in range(C):
                                last = pe.matmul(d[:, 0:2 * P], wx[:, f, P * i:P * i + P], x1T[:, f, :],
                                                 start=f == 0, stop=f == C - 1)
                            last.then_inc(dense_ready, 1)
                        elif kind == "x1n":
                            if i == 0 and p == BLOCKS - 1:
                                wait_copied(pe, p, r, "proj", C - 2)
                                wait_copied(pe, p, r, "proj", C - 1)
                            for f in range(C):
                                last = pe.transpose(d[:, P * f:P * f + P], x1T[:, f, P * i:P * i + P], ident[:])
                            last.then_inc(dense_ready, 1)
                        elif kind == "step":
                            before = (i - 1) % STEPS
                            d = rec_bank(p, i)
                            if p == BLOCKS:
                                if i % HALF == 0:
                                    pe.wait_ge(x1_set_out[i // HALF], r + 1)
                                pe.wait_ge(rec_turned, step_count(p, r, i) - 1)
                                for f in range(C):
                                    for j in range(C):
                                        pe.matmul(d[Q * j:Q * j + B, 0:P], x1step[:, i // HALF, f, :, i % HALF],
                                                  wx[:, f, :].rearrange("p (a j c) -> p a j c", a=C, j=C)[:, :, j, :],
                                                  start=f == 0, stop=False)
                            pe.wait_ge(h_ready, step_count(p, r, i) + 1)
                            for f in range(C):
                                for j in range(C):
                                    last = pe.matmul(d[Q * j:Q * j + B, 0:P], hist[:, before // HALF, f, :, before % HALF],
                                                     wh[:, f, P * j:P * j + P], start=f == 0 and p < BLOCKS,
                                                     stop=f == C - 1)
                            last.then_inc(rec_ready, 1)
                        elif kind == "out":
                            wait_bank(pe, p, r, "out", i)
                            pe.wait_ge(h_ready, r * STEPS + ((p - 1) * PAIRS * STEPS + (i + 1) * HALF + 1))
                            for f in range(C):
                                last = pe.transpose(bank(p, kind, i)[:, P * f:P * f + P],
                                                    hist[:, i, f, :, :].rearrange("p b s -> p (b s)"), ident[:])
                            last.then_inc(dense_ready, 1)


def kernel(x, cond_1024, mask_Bx1x1xS_ff0, L0_cond_c_attn_w, L0_cond_c_attn_b, L0_cond_c_proj_w,
           L0_cond_c_proj_b, L0_cond_uk_w, L0_cond_uk_b, L0_cond_uv_w, L0_cond_uv_b, L1_cond_Wx,
           L1_cond_Wh, L1_cond_b):
    import numpy as np
    import concourse.bacc as bacc
    from concourse.bass_utils import run_bass_kernel_spmd

    inputs = {
        "x": x, "cond": cond_1024, "mask": mask_Bx1x1xS_ff0, "w_qkv": L0_cond_c_attn_w,
        "w_proj": L0_cond_c_proj_w, "b_proj": L0_cond_c_proj_b,
        "uk_w": L0_cond_uk_w, "uk_b": L0_cond_uk_b, "uv_w": L0_cond_uv_w, "uv_b": L0_cond_uv_b,
        "w_x": L1_cond_Wx, "w_h": L1_cond_Wh, "b_h": L1_cond_b,
    }
    b_qkv = L0_cond_c_attn_b

    def folded(a, axis):
        axis %= a.ndim
        cut = a.reshape(a.shape[:axis] + (C, C, Q) + a.shape[axis + 1:])
        return np.swapaxes(cut, axis, axis + 1).reshape(a.shape)

    def chunked(a):
        return np.swapaxes(a.reshape((C, P) + a.shape[1:]), 0, 1)

    inputs["x"] = (folded(x, -1).reshape(PAIRS, 2, BLOCKS, P, C, P).transpose(2, 0, 5, 4, 1, 3)
                   .reshape(BLOCKS * PAIRS, P, C, 2 * P))
    inputs["cond"] = folded(cond_1024, -1)
    for name in ("w_qkv", "w_x", "w_h", "b_proj", "b_h"):
        inputs[name] = folded(inputs[name], 0)
    for name in ("w_proj", "w_x", "uk_w", "uv_w"):
        inputs[name] = folded(inputs[name], 1)
    for name in ("w_qkv", "w_proj", "w_x", "w_h", "uk_w", "uv_w", "uk_b", "b_proj", "b_h"):
        inputs[name] = chunked(inputs[name])
    inputs["b_qk"] = b_qkv[0:2 * D].reshape(2, C, P).transpose(2, 0, 1)
    inputs["b_v"] = b_qkv[2 * D:3 * D]
    arrays = {name: np.ascontiguousarray(a) for name, a in inputs.items()}
    arrays["ident_in"] = np.eye(P, dtype=np.float32)
    arrays["causal_in"] = (np.triu(np.ones((P, P)), 1) * (-10000.0 * ROOT)).astype(np.float32)
    arrays["headmask_in"] = (np.arange(D)[None, :] // DH == np.arange(P)[:, None] % H).astype(np.float32)

    nc = bacc.Bacc("TRN2", target_bir_lowering=False, num_devices=1)
    aps = {name: nc.dram_tensor(name, a.shape, mybir.dt.from_np(a.dtype), kind="ExternalInput").ap()
           for name, a in arrays.items()}
    out = nc.dram_tensor("out", (B, S, D), F32, kind="ExternalOutput").ap()
    attention_recurrence(nc, out=out, **aps)
    return run_bass_kernel_spmd(nc, [arrays], core_ids=[0]).results[0]["out"]
```
